# Optimizing a Trainium2 kernel written in Bass

```python
import numpy as np
import jax
import jax.numpy as jnp

def _softmax(x, axis=-1):
    return jax.nn.softmax(x, axis=axis)

def _gelu(x):
    return jax.nn.gelu(x, approximate=True)

def _silu(x):
    return jax.nn.silu(x)

def _sigmoid(x):
    return jax.nn.sigmoid(x)

def _layernorm(x, axis=-1, eps=1e-05):
    m = jnp.mean(x, axis=axis, keepdims=True)
    v = jnp.var(x, axis=axis, keepdims=True)
    return (x - m) / jnp.sqrt(v + eps)

def _scatter_add(tgt, idx, src, axis=0):
    return tgt.at[idx].add(src)

def _segment_sum(src, seg, n):
    return jax.ops.segment_sum(src, seg, n)
kernel_name = 'mk_gnn_resnorm_d2_gnn_r8_31c97c'

def setup_inputs(seed: int=0):
    np.random.seed(seed)
    _w = jnp.asarray

    def _rec_inputs():
        import jax
        import jax.numpy as jnp
        _gk = jax.random.key(seed)
        x = -0.000202 + 1 * jax.random.normal(jax.random.fold_in(_gk, 1), (12500, 64), jnp.float32)
        src = jax.random.randint(jax.random.fold_in(_gk, 2), (400000,), 0, 12500, jnp.int32)
        dst = jnp.minimum((12500 * jax.random.uniform(jax.random.fold_in(_gk, 3), (400000,)) ** 2.0).astype(jnp.int32), 99999)
        _o = jnp.argsort(dst, stable=True)
        src = src[_o]
        dst = dst[_o]
        edge_attr_64 = 7.68618e-05 + 1.00005 * jax.random.normal(jax.random.fold_in(_gk, 12), (400000, 64), jnp.float32)
        return (x, src, dst, edge_attr_64)
    x, src, dst, edge_attr_64 = _rec_inputs()

    def _L0_gnn_setup():
        import jax, jax.numpy as jnp
        import numpy as np
        EPS = 1e-05

        def _mlp(h, W, b, gamma, beta):
            h = h @ W + b
            mu = jnp.mean(h, axis=0)
            var = jnp.var(h, axis=0)
            h = (h - mu) * jax.lax.rsqrt(var + EPS) * gamma + beta
            return h * jax.nn.sigmoid(h)
        key = jax.random.key(seed)
        ks = jax.random.split(key, 10)
        N, E, D, G = (12500, 125000, 64, 16)
        x = jax.random.normal(ks[0], (N, D), dtype=jnp.float32)
        edge_index = jax.random.randint(ks[1], (2, E), 0, N, dtype=jnp.int64)
        edge_attr = jax.random.normal(ks[2], (E, D), dtype=jnp.float32)
        u = jax.random.normal(ks[3], (G, D), dtype=jnp.float32)
        batch = jax.random.randint(ks[4], (N,), 0, G, dtype=jnp.int64)
        s1 = 1.0 / np.sqrt(2 * D)
        W1 = jax.random.uniform(ks[5], (2 * D, D), jnp.float32, -s1, s1)
        b1 = jax.random.uniform(ks[6], (D,), jnp.float32, -s1, s1)
        W2 = jax.random.uniform(ks[7], (2 * D, D), jnp.float32, -s1, s1)
        b2 = jax.random.uniform(ks[8], (D,), jnp.float32, -s1, s1)
        g1 = jnp.ones((D,), jnp.float32)
        be1 = jnp.zeros((D,), jnp.float32)
        g2 = jnp.ones((D,), jnp.float32)
        be2 = jnp.zeros((D,), jnp.float32)
        return {'x': x, 'edge_attr': edge_attr, 'u': u, 'W1': W1, 'b1': b1, 'g1': g1, 'be1': be1, 'W2': W2, 'b2': b2, 'g2': g2, 'be2': be2, 'edge_index': edge_index, 'batch': batch}
    _L0_gnn_all = _L0_gnn_setup()
    _L0_gnn_in = {k: v for k, v in _L0_gnn_all.items() if k in ('u', 'W1', 'b1', 'g1', 'be1', 'W2', 'b2', 'g2', 'be2')}
    del _L0_gnn_all

    def _L1_gnn_setup():
        import jax, jax.numpy as jnp
        import numpy as np
        N_NODES = 12500
        N_EDGES = 125000
        D_IN = 64
        D_OUT = 64
        key = jax.random.key(seed)
        k_x, k_ei, k_ea, k_w, k_b = jax.random.split(key, 5)
        x = jax.random.normal(k_x, (N_NODES, D_IN), dtype=jnp.float32)
        edge_index = jax.random.randint(k_ei, (2, N_EDGES), 0, N_NODES, dtype=jnp.int64)
        edge_attr = jax.random.normal(k_ea, (N_EDGES, D_IN), dtype=jnp.float32)
        bound = 1.0 / np.sqrt(D_IN)
        W = jax.random.uniform(k_w, (D_OUT, D_IN), dtype=jnp.float32, minval=-bound, maxval=bound)
        b = jax.random.uniform(k_b, (D_OUT,), dtype=jnp.float32, minval=-bound, maxval=bound)
        eps = jnp.zeros((), dtype=jnp.float32)
        return {'x': x, 'edge_index': edge_index, 'edge_attr': edge_attr, 'W': W, 'b': b, 'eps': eps}
    _L1_gnn_all = _L1_gnn_setup()
    _L1_gnn_in = {k: v for k, v in _L1_gnn_all.items() if k in ('W', 'b', 'eps')}
    del _L1_gnn_all
    return {'x': x, 'src': src, 'dst': dst, 'edge_attr_64': edge_attr_64, 'L0_gnn_u': _L0_gnn_in['u'], 'L0_gnn_W1': _L0_gnn_in['W1'], 'L0_gnn_b1': _L0_gnn_in['b1'], 'L0_gnn_g1': _L0_gnn_in['g1'], 'L0_gnn_be1': _L0_gnn_in['be1'], 'L0_gnn_W2': _L0_gnn_in['W2'], 'L0_gnn_b2': _L0_gnn_in['b2'], 'L0_gnn_g2': _L0_gnn_in['g2'], 'L0_gnn_be2': _L0_gnn_in['be2'], 'L1_gnn_W': _L1_gnn_in['W'], 'L1_gnn_b': _L1_gnn_in['b'], 'L1_gnn_eps': _L1_gnn_in['eps']}

def reference(x, src, dst, edge_attr_64, L0_gnn_u, L0_gnn_W1, L0_gnn_b1, L0_gnn_g1, L0_gnn_be1, L0_gnn_W2, L0_gnn_b2, L0_gnn_g2, L0_gnn_be2, L1_gnn_W, L1_gnn_b, L1_gnn_eps):
    import jax
    import jax.numpy as jnp

    def _L0_gnn_ref(x, edge_attr, u, W1, b1, g1, be1, W2, b2, g2, be2, edge_index, batch):
        import jax, jax.numpy as jnp
        import numpy as np
        EPS = 1e-05

        def _mlp(h, W, b, gamma, beta):
            h = h @ W + b
            mu = jnp.mean(h, axis=0)
            var = jnp.var(h, axis=0)
            h = (h - mu) * jax.lax.rsqrt(var + EPS) * gamma + beta
            return h * jax.nn.sigmoid(h)
        N = x.shape[0]
        row, col = (edge_index[0], edge_index[1])
        msg = _mlp(jnp.concatenate([x[row], edge_attr], axis=1), W1, b1, g1, be1)
        sums = jax.ops.segment_sum(msg, col, num_segments=N)
        cnt = jax.ops.segment_sum(jnp.ones((msg.shape[0],), msg.dtype), col, num_segments=N)
        agg = sums / jnp.maximum(cnt, 1.0)[:, None]
        return _mlp(jnp.concatenate([x, agg], axis=1), W2, b2, g2, be2)

    def _L1_gnn_ref(x, edge_index, edge_attr, W, b, eps):
        import jax, jax.numpy as jnp
        import numpy as np
        N_NODES = 12500
        N_EDGES = 125000
        D_IN = 64
        D_OUT = 64
        src = edge_index[0]
        dst = edge_index[1]
        msg = jax.nn.relu(x[src] + edge_attr)
        agg = jax.ops.segment_sum(msg, dst, num_segments=x.shape[0])
        h = (1.0 + eps) * x + agg
        out = h @ W.T + b
        return jax.nn.relu(out)
    edge_index = jnp.stack([src, dst])
    batch0 = jnp.zeros((12500,), jnp.int32)
    x = _layernorm(x + _L0_gnn_ref(x, edge_attr_64, L0_gnn_u, L0_gnn_W1, L0_gnn_b1, L0_gnn_g1, L0_gnn_be1, L0_gnn_W2, L0_gnn_b2, L0_gnn_g2, L0_gnn_be2, edge_index, batch0), axis=-1)
    x = _layernorm(x + _L1_gnn_ref(x, edge_index, edge_attr_64, L1_gnn_W, L1_gnn_b, L1_gnn_eps), axis=-1)
    return x

_drawn_inputs = setup_inputs


def setup_inputs(seed=0):
    import zlib

    import numpy as np

    out = dict(_drawn_inputs(seed))
    spreads = {'L0_gnn_g1': (1.0, 0.6),
     'L0_gnn_be1': (0.0, 0.8),
     'L0_gnn_g2': (1.0, 0.2),
     'L0_gnn_be2': (0.0, 0.1)}
    factors = {'L0_gnn_b1': 8.0, 'L0_gnn_b2': 8.0, 'L1_gnn_b': 4.567}
    for name, (base, spread) in spreads.items():
        noise = np.random.default_rng([zlib.crc32(name.encode()), seed]).standard_normal(out[name].shape)
        drawn = base * np.exp(spread * noise) if base else spread * noise
        out[name] = jnp.asarray(drawn.astype(out[name].dtype))
    for name, factor in factors.items():
        out[name] = (out[name] * factor).astype(out[name].dtype)
    return out
```

```python
import concourse.bass as bass
from concourse import mybir
from contextlib import ExitStack



class Chain:

    def __init__(self, engine, sem, base=0):
        self.engine, self.sem, self.base, self.n = engine, sem, base, 0

    def link(self, instruction):
        self.n += 1
        instruction.then_inc(self.sem, 1)
        self.engine.wait_ge(self.sem, self.base + self.n)


def gnn_kernel(nc, x, src, dst, edge, W1, b1, g1, be1, W2, b2, g2, be2, W3, b3, eps1, out):
    fp32 = mybir.dt.float32
    int32 = mybir.dt.int32
    ALU = mybir.AluOpType
    ACT = mybir.ActivationFunctionType
    AX = mybir.AxisListType.X
    ds = bass.ds

    P = 128
    NODES, D = x.shape
    EDGES = edge.shape[0]
    EPS = 1e-5
    TG = 5
    EG = TG * P
    S = 5
    G = EDGES // EG
    SB = G // S
    WIN = 64
    NW = -(-NODES // WIN)
    HC = TG * D
    NP = 125
    NT = NODES // NP
    CT = 4
    CN = CT * NP
    PT = S * CT
    PIECES = NT // PT
    CHUNKS = NT // CT
    assert EDGES == G * EG and G == SB * S and SB <= P and NODES == NP * NT and NT == PIECES * PT

    edge_v = edge.rearrange("(g p j) c -> g p j c", p=P, j=TG)
    src_v = src.rearrange("(sb n) -> sb n", sb=SB)
    dst_v = dst.rearrange("(sb n) -> sb n", sb=SB)
    first_v = dst.rearrange("(o g n) -> o g n", o=1, n=EG)[:, :, 0]
    x_v = x.rearrange("(p t) c -> p t c", p=NP)
    out_v = out.rearrange("(p t) c -> p (t c)", p=NP)
    h_dram = nc.dram_tensor("h_scratch", (G, P, HC), fp32, kind="Internal").ap()
    x1_dram = nc.dram_tensor("x1_scratch", (NODES, D), fp32, kind="Internal").ap()
    x1_v = x1_dram.rearrange("(p t) c -> p (t c)", p=NP)

    def col(v):
        return v.rearrange("(a b) -> a b", b=1)

    ctx = ExitStack()
    with ctx:
        def sb(where, name, shape, dt=fp32):
            return where.enter_context(nc.sbuf_tensor(name, shape, dt))

        in_use = []

        def sem(name):
            in_use.append(nc.alloc_semaphore(name))
            return in_use[-1]

        def sems(name):
            return [sem(f"{name}{s}") for s in range(S)]

        def clear_semaphores():
            nc.clear_and_free_semaphores(list(in_use))
            nc.all_engine_barrier()
            in_use.clear()

        steps = ctx.enter_context(nc.semaphore("steps"))

        def carry_wait(engine):
            engine.sem_inc(steps, 1)

        gathered_x = [ctx.enter_context(nc.semaphore(f"gathered_x{s}")) for s in range(S)]
        gathered_x1 = [ctx.enter_context(nc.semaphore(f"gathered_x1{s}")) for s in range(S)]
        gathered_general = ctx.enter_context(nc.semaphore("gathered_general"))

        table = sb(ctx, "table", [P, NODES + WIN])
        x_nodes = sb(ctx, "x_nodes", [NP, NT * D])
        src_idx = sb(ctx, "src_idx", [P, (SB + 1) * S * TG], int32)
        rel5 = sb(ctx, "rel5", [P, G, TG])
        rel6 = sb(ctx, "rel6", [P, G, 6])
        base_all = sb(ctx, "base_all", [P, G])
        base_row = sb(ctx, "base_row", [1, G], int32)
        idx_ring = sb(ctx, "idx_ring", [P, S, TG], int32)
        ident = sb(ctx, "ident", [P, P])
        halves = sb(ctx, "halves", [P, P])
        window = sb(ctx, "window", [P, WIN])
        flag = sb(ctx, "flag", [1, 1], int32)
        W1_sb = sb(ctx, "W1_sb", [2 * D, D])
        W2_sb = sb(ctx, "W2_sb", [2 * D, D])
        W3T = sb(ctx, "W3T", [D, 2 * D])
        b1c = sb(ctx, "b1c", [P, 1])
        g1c = sb(ctx, "g1c", [P, 1])
        be1c = sb(ctx, "be1c", [P, 1])
        b2c = sb(ctx, "b2c", [D, 1])
        g2c = sb(ctx, "g2c", [D, 1])
        be2c = sb(ctx, "be2c", [D, 1])
        b3c = sb(ctx, "b3c", [D, 1])
        eps_c = sb(ctx, "eps_c", [D, 1])
        scale1 = sb(ctx, "scale1", [P, 1])
        shift1 = sb(ctx, "shift1", [P, 1])
        scale2 = sb(ctx, "scale2", [D, 1])
        shift2 = sb(ctx, "shift2", [D, 1])
        epsP = sb(ctx, "epsP", [P, 1])
        PS = ctx.enter_context(nc.psum_tensor("PS", [P, 8, 512], fp32))

        def banks(first, n, parts, cols):
            return PS[0:parts, first:first + n, :].rearrange("p b c -> p (b c)")[:, 0:cols]

        x3 = x_nodes[:, :].rearrange("p (t c) -> p t c", c=D)
        table_t = table[:, 0:NODES].rearrange("f (p t) -> f t p", t=NT)
        idx_flat = idx_ring[:, :, :].rearrange("p s j -> p (s j)")

        with ExitStack() as here:
            src_rows = sb(here, "src_rows", [SB, S * EG], int32)
            dst_rows = sb(here, "dst_rows", [SB, S * EG], int32)
            iota_i = sb(here, "iota_i", [P, WIN], int32)
            base_f = sb(here, "base_f", [1, G])
            ones_row = sb(here, "ones_row", [1, P])
            ones_col = sb(here, "ones_col", [P, 1])
            W3_sb = sb(here, "W3_sb", [D, D])
            most = sb(here, "most", [P, 1])
            least = sb(here, "least", [P, 1])
            bad = sb(here, "bad", [P, 1])
            flag_f = sb(here, "flag_f", [1, 1])
            src_f = src_rows[:, :].bitcast(fp32)
            dst_f = dst_rows[:, :].bitcast(fp32)
            srcT = src_f.rearrange("sb (q p j) -> sb q j p", q=S, j=TG)
            dstT = dst_f.rearrange("sb (q p j) -> sb q j p", q=S, j=TG)

            s_src = sem("s_src")
            s_dst = sem("s_dst")
            s_first = sem("s_first")
            s_x = sem("s_x")
            s_w = sem("s_w")
            s_zero = sem("s_zero")
            s_ident = sem("s_ident")
            s_iota = sem("s_iota")
            s_const = sem("s_const")
            src_float = sem("src_float")
            dst_float = sem("dst_float")
            first_float = sem("first_float")
            pieces_put = sem("pieces_put")
            pieces_taken = sem("pieces_taken")
            base_put = sem("base_put")
            w3_put = sem("w3_put")
            bad_ready = sem("bad_ready")
            bad_sum = sem("bad_sum")
            prep_chain = sem("prep_chain")

            with nc.Block() as block:
                @block.sync
                def _(sp):
                    sp.dma_start(src_rows[:, :], src_v).then_inc(s_src, 16)
                    sp.dma_start(dst_rows[:, :], dst_v).then_inc(s_dst, 16)
                    sp.dma_start(base_row[:, :], first_v, allow_slow_non_contiguous=True).then_inc(s_first, 16)
                    sp.dma_start(x_nodes[:, :], x_v.rearrange("p t c -> p (t c)")).then_inc(s_x, 16)
                    sp.wait_ge(s_x, 16)

                @block.scalar
                def _(act):
                    for to, of in ((W3_sb[:, :], W3), (W1_sb[:, :], W1), (W2_sb[:, :], W2),
                                   (b1c[0:D, :], col(b1)), (b1c[D:P, :], col(b1)),
                                   (g1c[0:D, :], col(g1)), (g1c[D:P, :], col(g1)),
                                   (be1c[0:D, :], col(be1)), (be1c[D:P, :], col(be1)),
                                   (b2c[:, :], col(b2)), (g2c[:, :], col(g2)), (be2c[:, :], col(be2)),
                                   (b3c[:, :], col(b3)), (eps_c[:, :], eps1.partition_broadcast(D))):
                        act.dma_start(to, of).then_inc(s_w, 16)
                    act.wait_ge(s_w, 16 * 14)

                @block.gpsimd
                def _(pool):
                    nc.gpsimd.memset(ident[:, :], 0.0).then_inc(s_zero, 1)
                    pool.wait_ge(s_zero, 1)
                    nc.gpsimd.affine_select(out=ident[:, :], in_=ident[:, :], compare_op=ALU.not_equal,
                                            fill=1.0, base=0, pattern=[[-1, P]],
                                            channel_multiplier=1).then_inc(s_ident, 1)
                    nc.gpsimd.memset(ones_row[:, :], 1.0)
                    nc.gpsimd.memset(ones_col[:, :], 1.0)
                    nc.gpsimd.memset(epsP[:, :], EPS)
                    nc.gpsimd.memset(src_idx[:, G * TG:], 0).then_inc(s_const, 1)
                    nc.gpsimd.iota(iota_i[:, :], pattern=[[1, WIN]], base=0,
                                   channel_multiplier=0).then_inc(s_iota, 1)
                    pool.wait_ge(s_iota, 1)
                    nc.gpsimd.tensor_copy(window[:, :], iota_i[:, :]).then_inc(s_const, 1)

                @block.tensor
                def _(pe):
                    pe.wait_ge(s_ident, 1)
                    for n in range(2 * S):
                        rows, q = (srcT, n) if n < S else (dstT, n - S)
                        if n == 0:
                            pe.wait_ge(src_float, 1)
                        if n == S:
                            pe.wait_ge(dst_float, 1)
                        if n >= 2:
                            pe.wait_ge(pieces_taken, n - 1)
                        for j in range(TG):
                            to = banks(2 * (n % 2), 2, P, TG * P)[:, j * P:j * P + SB]
                            last = nc.tensor.transpose(to, rows[:, q, j, :], ident[0:SB, 0:SB])
                        last.then_inc(pieces_put, 1)
                    pe.wait_ge(first_float, 1)
                    pe.wait_ge(s_const, 1)
                    for c in range(0, G, 512):
                        n = min(512, G - c)
                        last = nc.tensor.matmul(PS[:, 4 + c // 512, 0:n], ones_row[:, :],
                                                base_f[0:1, c:c + n], start=True, stop=True)
                    last.then_inc(base_put, 1)
                    pe.wait_ge(s_w, 16 * 14)
                    nc.tensor.transpose(PS[0:D, 6, 0:D], W3_sb[:, :], ident[0:D, 0:D]).then_inc(w3_put, 1)
                    pe.wait_ge(bad_ready, 1)
                    nc.tensor.matmul(PS[0:1, 7, 0:1], bad[:, :], ones_col[:, :], start=True,
                                     stop=True).then_inc(bad_sum, 1)

                @block.vector
                def _(dve):
                    chain = Chain(dve, prep_chain)
                    nc.vector.memset(rel6[D:P, :, 4:6], -1.0)
                    dve.wait_ge(s_src, 16)
                    nc.vector.tensor_copy(src_f, src_rows[:, :]).then_inc(src_float, 1)
                    dve.wait_ge(s_dst, 16)
                    nc.vector.tensor_copy(dst_f, dst_rows[:, :]).then_inc(dst_float, 1)
                    dve.wait_ge(s_first, 16)
                    nc.vector.tensor_copy(base_f[:, :], base_row[:, :]).then_inc(first_float, 1)
                    dve.wait_ge(s_const, 1)
                    for n in range(2 * S):
                        to, q = (src_idx[:, 0:G * TG], n) if n < S else \
                            (rel5[:, :, :].rearrange("p g j -> p (g j)"), n - S)
                        dve.wait_ge(pieces_put, n + 1)
                        put = banks(2 * (n % 2), 2, P, TG * P).rearrange("p (j c) -> p j c", j=TG)
                        last = nc.vector.tensor_copy(
                            to.rearrange("p (sb q j) -> p q j sb", q=S, j=TG)[:, q, :, :], put[:, :, 0:SB])
                        last.then_inc(pieces_taken, 1)
                    dve.wait_ge(pieces_taken, 2 * S)
                    chain.link(nc.vector.tensor_copy(idx_flat, src_idx[:, 0:S * TG]))
                    dve.wait_ge(base_put, 1)
                    chain.link(nc.vector.tensor_copy(base_all[:, :], banks(4, 2, P, G)))
                    chain.link(nc.vector.tensor_tensor(
                        rel5[:, :, :], rel5[:, :, :],
                        base_all[:, :].unsqueeze(2).to_broadcast([P, G, TG]), ALU.subtract))
                    nc.vector.tensor_copy(rel6[:, :, 0:2], rel5[:, :, 0:4:2])
                    nc.vector.tensor_copy(rel6[:, :, 2:4], rel5[:, :, 1:4:2])
                    nc.vector.tensor_copy(rel6[0:D, :, 4:5], rel5[0:D, :, 4:5])
                    nc.vector.tensor_copy(rel6[0:D, :, 5:6], rel5[D:P, :, 4:5])
                    rel_flat = rel5[:, :, :].rearrange("p g j -> p (g j)")
                    nc.vector.reduce_max(most[:, :], rel_flat, AX)
                    chain.link(nc.vector.tensor_reduce(least[:, :], rel_flat, AX, ALU.min))
                    chain.link(nc.vector.tensor_scalar(most[:, :], most[:, :], float(WIN - 1), None, ALU.is_gt))
                    chain.link(nc.vector.tensor_scalar(least[:, :], least[:, :], 0.0, None, ALU.is_lt))
                    nc.vector.tensor_tensor(bad[:, :], most[:, :], least[:, :], ALU.add).then_inc(bad_ready, 1)
                    dve.wait_ge(bad_sum, 1)
                    chain.link(nc.vector.tensor_scalar(flag_f[:, :], PS[0:1, 7, 0:1], 0.0, None, ALU.is_gt))
                    nc.vector.tensor_copy(flag[:, :], flag_f[:, :])
                    dve.wait_ge(w3_put, 1)
                    for c in (0, D):
                        nc.vector.tensor_copy(W3T[:, c:c + D], PS[0:D, 6, 0:D])
                    for c in (0, D):
                        last = nc.vector.tensor_tensor(halves[:, c:c + D], ident[:, 0:D], ident[:, D:P], ALU.add)
                    chain.link(last)
                    nc.vector.tensor_scalar(halves[:, :], halves[:, :], 0.5, None, ALU.mult)
                    nc.vector.memset(table[:, :], 0.0)

        with ExitStack() as here:
            Z = sb(here, "Z", [P, S, TG, 2 * D])
            ZT = sb(here, "ZT", [P, EG])
            h_ring = sb(here, "h_ring", [P, S, HC])
            stats = sb(here, "stats", [P, G * 6])
            moments = sb(here, "moments", [P, 2])
            mean = sb(here, "mean", [P, 1])
            off = sb(here, "off", [P, 1])
            var = sb(here, "var", [P, 1])

            e_loaded = sems("e_loaded")
            gathered = gathered_x
            rows_done = sems("rows_done")
            zt_taken = sem("zt_taken")
            h_put = sem("h_put")
            h_ready = sems("h_ready")
            h_stored = sems("h_stored")
            stats_done = sems("stats_done")
            idx_ready = sems("idx_ready")
            mean_in = sem("mean_in")
            mean_put = sem("mean_put")
            var_in = sem("var_in")
            var_put = sem("var_put")
            var_sb = sem("var_sb")
            root1 = sem("root1")
            a_chain = sem("a_chain")

            with nc.Block() as block:
                @block.sync
                def _(sp):
                    with sp.Fori(0, SB) as i:
                        for s in range(S):
                            sp.wait_ge(rows_done[s], i)
                            sp.dma_start(Z[:, s, :, D:2 * D], edge_v[i * S + s]).then_inc(e_loaded[s], 16)

                @block.gpsimd
                def _(pool):
                    with pool.Fori(0, SB) as i:
                        for s in range(S):
                            pool.wait_ge(idx_ready[s], i)
                            pool.wait_ge(rows_done[s], i)
                            carry_wait(pool)
                            for j in range(TG):
                                nc.gpsimd.indirect_dma_start(
                                    out=Z[:, s, j, 0:D], out_offset=None, in_=x,
                                    in_offset=bass.IndirectOffsetOnAxis(ap=idx_ring[:, s, j:j + 1], axis=0)
                                ).then_inc(gathered[s], 16)

                @block.tensor
                def _(pe):
                    with pe.Fori(0, SB) as i:
                        for s in range(S):
                            g = i * S + s
                            rows_at = 2 * (s % 2)
                            pe.wait_ge(zt_taken, i * S if s < 2 else g - 1)
                            pe.wait_ge(e_loaded[s], i * 16 + 16)
                            pe.wait_ge(gathered[s], i * (16 * TG) + 16 * TG)
                            for j in range(TG):
                                last = nc.tensor.transpose(banks(rows_at, 2, P, EG)[:, j * P:(j + 1) * P],
                                                           Z[:, s, j, :], ident[:, :])
                            last.then_inc(rows_done[s], 1)
                            pe.wait_ge(zt_taken, g + 1)
                            h = PS[:, 4 + s % 2, 0:HC]
                            for half in (0, 1):
                                lo = half * D
                                nc.tensor.matmul(h[lo:lo + D, 0:2 * P], W1_sb[:, :],
                                                 ZT[:, half * 2 * P:(half + 1) * 2 * P], start=True, stop=True)
                                last = nc.tensor.matmul(h[lo:lo + D, 2 * P:HC], W1_sb[:, :],
                                                        ZT[:, 4 * P + lo:4 * P + lo + D], start=True, stop=True)
                            last.then_inc(h_put, 1)
                    pe.wait_ge(mean_in, 1)
                    nc.tensor.matmul(PS[:, 6, 0:1], halves[:, :], moments[:, 0:1], start=True,
                                     stop=True).then_inc(mean_put, 1)
                    pe.wait_ge(var_in, 1)
                    nc.tensor.matmul(PS[:, 7, 0:1], halves[:, :], var[:, :], start=True,
                                     stop=True).then_inc(var_put, 1)

                @block.scalar
                def _(act):
                    with act.Fori(0, SB) as i:
                        for s in range(S):
                            g = i * S + s
                            act.wait_ge(rows_done[s], i + 1)
                            act.activation(ZT[:, :], banks(2 * (s % 2), 2, P, EG), ACT.Copy).then_inc(zt_taken, 1)
                            act.wait_ge(h_put, g + 1)
                            act.wait_ge(h_stored[s], i * 16)
                            act.wait_ge(stats_done[s], i)
                            act.activation(h_ring[:, s, :], PS[:, 4 + s % 2, 0:HC], ACT.Identity,
                                           bias=b1c[:, :]).then_inc(h_ready[s], 1)
                            act.wait_ge(h_ready[s], i + 1)
                            act.dma_start(h_dram[g], h_ring[:, s, :]).then_inc(h_stored[s], 16)
                    act.wait_ge(var_sb, 1)
                    act.activation(var[:, :], var[:, :], ACT.Sqrt, bias=epsP[:, :]).then_inc(root1, 1)
                    for s in range(S):
                        act.wait_ge(h_stored[s], 16 * SB)

                @block.vector
                def _(dve):
                    with dve.Fori(0, SB) as i:
                        for s in range(S):
                            dve.wait_ge(h_ready[s], i + 1)
                            nc.vector.bn_stats(stats[:, ds(i * (6 * S) + 6 * s, 6)],
                                               h_ring[:, s, :]).then_inc(stats_done[s], 1)
                            nc.vector.tensor_copy(idx_ring[:, s, :],
                                                  src_idx[:, ds(i * (S * TG) + (S + s) * TG, TG)]
                                                  ).then_inc(idx_ready[s], 1)
                    chain = Chain(dve, a_chain)
                    dve.wait_ge(stats_done[S - 1], SB)
                    nc.vector.bn_aggr(moments[:, :], stats[:, :]).then_inc(mean_in, 1)
                    dve.wait_ge(mean_put, 1)
                    chain.link(nc.vector.tensor_copy(mean[:, :], PS[:, 6, 0:1]))
                    chain.link(nc.vector.tensor_tensor(off[:, :], moments[:, 0:1], mean[:, :], ALU.subtract))
                    chain.link(nc.vector.tensor_tensor(off[:, :], off[:, :], off[:, :], ALU.mult))
                    nc.vector.tensor_tensor(var[:, :], moments[:, 1:2], off[:, :], ALU.add).then_inc(var_in, 1)
                    dve.wait_ge(var_put, 1)
                    nc.vector.tensor_copy(var[:, :], PS[:, 7, 0:1]).then_inc(var_sb, 1)
                    dve.wait_ge(root1, 1)
                    chain.link(nc.vector.reciprocal(scale1[:, :], var[:, :]))
                    chain.link(nc.vector.tensor_tensor(scale1[:, :], scale1[:, :], g1c[:, :], ALU.mult))
                    chain.link(nc.vector.tensor_tensor(off[:, :], mean[:, :], scale1[:, :], ALU.mult))
                    nc.vector.tensor_tensor(shift1[:, :], be1c[:, :], off[:, :], ALU.subtract)

        clear_semaphores()

        def pass_b(here):
            h_ring = sb(here, "hb_ring", [P, S, HC])
            m_ring = sb(here, "m_ring", [P, S, HC])
            msg = sb(here, "msg", [P, S, 6, 2 * D])
            hot = sb(here, "hot", [P, S, 6, WIN])

            h_loaded = sems("h_loaded")
            silu_done = sems("silu_done")
            turned = sems("turned")
            msg_ready = sems("msg_ready")
            hot_ready = sems("hot_ready")
            summed = sems("summed")
            added = sem("added")
            b_const = sem("b_const")

            def bank_t(s):
                return s % 3

            def bank_o(s):
                return 3 + s % 3

            with nc.Block() as block:
                @block.sync
                def _(sp):
                    with sp.Fori(0, SB) as i:
                        for s in range(S):
                            sp.wait_ge(silu_done[s], i)
                            sp.dma_start(h_ring[:, s, :], h_dram[i * S + s]).then_inc(h_loaded[s], 16)

                @block.gpsimd
                def _(pool):
                    nc.gpsimd.memset(msg[:, :, :, 0:D], 1.0).then_inc(b_const, 1)

                @block.scalar
                def _(act):
                    def silu(i, s):
                        act.wait_ge(h_loaded[s], i * 16 + 16)
                        act.wait_ge(turned[s], i)
                        act.activation(m_ring[:, s, :], h_ring[:, s, :], ACT.Silu, bias=shift1[:, :],
                                       scale=scale1[:, :]).then_inc(silu_done[s], 1)

                    def take(i, s):
                        act.wait_ge(turned[s], i + 1)
                        act.wait_ge(summed[s], i)
                        act.activation(msg[:, s, :, D:2 * D],
                                       PS[:, bank_t(s), 0:6 * D].rearrange("p (t c) -> p t c", c=D),
                                       ACT.Copy).then_inc(msg_ready[s], 1)

                    act.wait_ge(b_const, 2)
                    silu(0, 0)
                    with act.Fori(0, SB - 1) as i:
                        for s in range(S):
                            silu(i + (s + 1) // S, (s + 1) % S)
                            take(i, s)
                    for s in range(S):
                        if s + 1 < S:
                            silu(SB - 1, s + 1)
                        take(SB - 1, s)

                @block.tensor
                def _(pe):
                    def turn(i, s):
                        pe.wait_ge(silu_done[s], i + 1)
                        if s >= 3:
                            pe.wait_ge(msg_ready[s - 3], i + 1)
                        else:
                            pe.wait_ge(msg_ready[s + 3 if s < 2 else s], i)
                        for c, (at, n) in enumerate(((0, P), (P, P), (2 * P, D))):
                            last = nc.tensor.transpose(PS[0:n, bank_t(s), c * P:(c + 1) * P],
                                                       m_ring[:, s, at:at + n], ident[:, :])
                        last.then_inc(turned[s], 1)

                    def products(i, s):
                        pe.wait_ge(msg_ready[s], i + 1)
                        pe.wait_ge(hot_ready[s], i + 1)
                        pe.wait_ge(added, i * S + max(s - 2, 0))
                        for t in range(6):
                            k = P if t < 4 else D
                            last = nc.tensor.matmul(PS[:, bank_o(s), 0:WIN], msg[0:k, s, t, :], hot[0:k, s, t, :],
                                                    start=(t == 0), stop=(t == 5))
                        last.then_inc(summed[s], 1)

                    pe.wait_ge(b_const, 2)
                    turn(0, 0)
                    with pe.Fori(0, SB - 1) as i:
                        for s in range(S):
                            turn(i + (s + 1) // S, (s + 1) % S)
                            products(i, s)
                    for s in range(S):
                        if s + 1 < S:
                            turn(SB - 1, s + 1)
                        products(SB - 1, s)

                @block.vector
                def _(dve):
                    def one_hot(i, s):
                        dve.wait_ge(summed[s], i)
                        nc.vector.tensor_tensor(
                            hot[:, s, :, :], window[:, :].unsqueeze(1).to_broadcast([P, 6, WIN]),
                            rel6[:, ds(i * S + s, 1), :].rearrange("p a t -> p (a t)").unsqueeze(2)
                            .to_broadcast([P, 6, WIN]), ALU.is_equal).then_inc(hot_ready[s], 1)

                    def add(i, s):
                        first = dve.value_load(base_row[0:1, ds(i * S + s, 1)], min_val=0, max_val=NODES - 1)
                        dve.wait_ge(summed[s], i + 1)
                        dve.wait_ge(added, i * S + s)
                        nc.vector.tensor_tensor(table[:, ds(first, WIN)], table[:, ds(first, WIN)],
                                                PS[:, bank_o(s), 0:WIN], ALU.add).then_inc(added, 1)

                    nc.vector.memset(PS[:, 0:3, :], 0.0).then_inc(b_const, 1)
                    one_hot(0, 0)
                    with dve.Fori(0, SB - 1) as i:
                        for s in range(S):
                            one_hot(i + (s + 1) // S, (s + 1) % S)
                            add(i, s)
                    for s in range(S):
                        if s + 1 < S:
                            one_hot(SB - 1, s + 1)
                        add(SB - 1, s)

        with ExitStack() as here:
            pass_b(here)

        def outside(dve, chain, cur, rel, base, parts):
            one = cur[:, 1, :]
            chain.link(nc.vector.tensor_scalar(cur[:, 0, :], rel, 0.0, None, ALU.is_lt))
            chain.link(nc.vector.tensor_scalar(one, rel, float(WIN - 1), None, ALU.is_gt))
            chain.link(nc.vector.tensor_tensor(cur[:, 0, :], cur[:, 0, :], one, ALU.add))
            chain.link(nc.vector.tensor_scalar(one, rel, base, 1.0, ALU.add, ALU.add))
            chain.link(nc.vector.tensor_tensor(cur[:, 0, :], cur[:, 0, :], one, ALU.mult))
            chain.link(nc.vector.tensor_scalar(cur[:, 0, :], cur[:, 0, :], -1.0, None, ALU.add))

        with ExitStack() as here:
            h_slot = sb(here, "h_slot", [P, HC])
            m_slot = sb(here, "m_slot", [P, HC])
            msg = sb(here, "msg_g", [P, 6, 2 * D])
            hot = sb(here, "hot_g", [P, 6, WIN])
            cur = sb(here, "cur_g", [P, 2, 6])
            h_in = sem("gb_h_in")
            silu_out = sem("gb_silu_out")
            turned = sem("gb_turned")
            msg_ready = sem("gb_msg_ready")
            hot_ready = sem("gb_hot_ready")
            summed = sem("gb_summed")
            added = sem("gb_added")
            moved_on = sem("gb_moved_on")
            gb_const = sem("gb_const")
            gb_chain = sem("gb_chain")
            with nc.Block() as block:
                @block.sync
                def _(sp):
                    with sp.If(sp.value_load(flag[0:1, 0:1], min_val=0, max_val=1) > 0):
                        with sp.Fori(0, G) as g:
                            sp.wait_ge(silu_out, g)
                            sp.dma_start(h_slot[:, :], h_dram[g]).then_inc(h_in, 16)

                @block.scalar
                def _(act):
                    with act.If(act.value_load(flag[0:1, 0:1], min_val=0, max_val=1) > 0):
                        act.wait_ge(gb_const, 2)
                        with act.Fori(0, G) as g:
                            act.wait_ge(h_in, g * 16 + 16)
                            act.wait_ge(turned, g)
                            act.activation(m_slot[:, :], h_slot[:, :], ACT.Silu, bias=shift1[:, :],
                                           scale=scale1[:, :]).then_inc(silu_out, 1)
                            act.wait_ge(turned, g + 1)
                            act.wait_ge(added, g * NW)
                            act.activation(msg[:, :, D:2 * D],
                                           PS[:, 0, 0:6 * D].rearrange("p (t c) -> p t c", c=D),
                                           ACT.Copy).then_inc(msg_ready, 1)

                @block.tensor
                def _(pe):
                    with pe.If(pe.value_load(flag[0:1, 0:1], min_val=0, max_val=1) > 0):
                        pe.wait_ge(gb_const, 2)
                        with pe.Fori(0, G) as g:
                            pe.wait_ge(silu_out, g + 1)
                            pe.wait_ge(msg_ready, g)
                            for c, (at, n) in enumerate(((0, P), (P, P), (2 * P, D))):
                                last = nc.tensor.transpose(PS[0:n, 0, c * P:(c + 1) * P],
                                                           m_slot[:, at:at + n], ident[:, :])
                            last.then_inc(turned, 1)
                            pe.wait_ge(msg_ready, g + 1)
                            carry_wait(pe)
                            with pe.Fori(0, NW) as w:
                                pe.wait_ge(hot_ready, g * NW + w + 1)
                                pe.wait_ge(added, g * NW + w)
                                for t in range(6):
                                    k = P if t < 4 else D
                                    last = nc.tensor.matmul(PS[:, 1, 0:WIN], msg[0:k, t, :], hot[0:k, t, :],
                                                            start=(t == 0), stop=(t == 5))
                                last.then_inc(summed, 1)

                @block.vector
                def _(dve):
                    with dve.If(dve.value_load(flag[0:1, 0:1], min_val=0, max_val=1) > 0):
                        nc.vector.memset(msg[:, :, 0:D], 1.0).then_inc(gb_const, 1)
                        nc.vector.memset(PS[:, 0, :], 0.0).then_inc(gb_const, 1)
                        with dve.Fori(0, G) as g:
                            chain = Chain(dve, gb_chain, g * 6)
                            dve.wait_ge(moved_on, g * NW)
                            outside(dve, chain, cur, rel6[:, ds(g, 1), :].rearrange("p a t -> p (a t)"),
                                    base_all[:, ds(g, 1)], P)
                            carry_wait(dve)
                            with dve.Fori(0, NW) as w:
                                dve.wait_ge(summed, g * NW + w)
                                dve.wait_ge(moved_on, g * NW + w)
                                nc.vector.tensor_tensor(
                                    hot[:, :, :], window[:, :].unsqueeze(1).to_broadcast([P, 6, WIN]),
                                    cur[:, 0, :].unsqueeze(2).to_broadcast([P, 6, WIN]),
                                    ALU.is_equal).then_inc(hot_ready, 1)
                                dve.wait_ge(hot_ready, g * NW + w + 1)
                                nc.vector.tensor_scalar(cur[:, 0, :], cur[:, 0, :], -float(WIN), None,
                                                        ALU.add).then_inc(moved_on, 1)
                                dve.wait_ge(summed, g * NW + w + 1)
                                dve.wait_ge(added, g * NW + w)
                                nc.vector.tensor_tensor(table[:, ds(w * WIN, WIN)], table[:, ds(w * WIN, WIN)],
                                                        PS[:, 1, 0:WIN], ALU.add).then_inc(added, 1)

        def layer_norm(chain, z, sq, small, to, root_in, root_out, n):
            mean, varc, rstd = small[:, 0, :], small[:, 1, :], small[:, 2, :]
            wide = [NP, PT, D]
            chain.link(nc.vector.reduce_sum(mean, z, AX))
            chain.link(nc.vector.tensor_scalar(mean, mean, 1.0 / D, None, ALU.mult))
            chain.link(nc.vector.tensor_tensor(z, z, mean.unsqueeze(2).to_broadcast(wide), ALU.subtract))
            chain.link(nc.vector.tensor_tensor(sq, z, z, ALU.mult))
            nc.vector.reduce_sum(varc, sq, AX).then_inc(root_in, 1)
            chain.engine.wait_ge(root_out, n + 1)
            chain.link(nc.vector.reciprocal(rstd, rstd))
            return nc.vector.tensor_tensor(to, z, rstd.unsqueeze(2).to_broadcast(wide), ALU.mult)

        LN_LINKS = 5

        clear_semaphores()

        with ExitStack() as here:
            x_ring = sb(here, "x_ring", [NP, S, CT, D])
            counts = sb(here, "counts", [P, NODES // 4])
            stats = sb(here, "stats_n", [D, CHUNKS * 6])
            moments = sb(here, "moments_n", [D, 2])
            root = sb(here, "root_n", [D, 1])
            act_ring = sb(here, "act_ring", [D, S, CN])
            z = sb(here, "z_n", [NP, PT, D])
            sq = sb(here, "sq_n", [NP, PT, D])
            small = sb(here, "small_n", [NP, 3, PT])
            x1 = sb(here, "x1_n", [NP, PT, D])
            eps1c = sb(here, "eps1c", [D, 1])

            x_loaded = sems("x_loaded")
            x_turned = sems("x_turned")
            counts_done = sem("counts_done")
            count_chain = sem("count_chain")
            xT_ready = sem("xT_ready")
            h2_put = sem("h2_put")
            h2_ready = sem("h2_ready")
            h2_stats = sem("h2_stats")
            n_chain = sem("n_chain")
            var2_in = sem("var2_in")
            root2 = sem("root2")
            bn2_ready = sem("bn2_ready")
            act_ready = sems("act_ready")
            act_turned = sems("act_turned")
            z_ready = sem("z_ready")
            ln_chain = sem("ln_chain")
            ln_in = sem("ln_in")
            ln_root = sem("ln_root")
            x1_ready = sem("x1_ready")
            x1_kept = sem("x1_kept")
            x1_stored = sem("x1_stored")
            x1_turned = sem("x1_turned")
            x1T_ready = sem("x1T_ready")
            eps_chain = sem("eps_chain")

            with nc.Block() as block:
                @block.sync
                def _(sp):
                    with sp.Fori(0, PIECES) as i:
                        for s in range(S):
                            sp.wait_ge(x_turned[s], i)
                            sp.dma_start(x_ring[:, s, :, :], x_v[:, ds((i * S + s) * CT, CT), :]
                                         ).then_inc(x_loaded[s], 16)
                    with sp.Fori(0, PIECES) as i:
                        sp.wait_ge(x1_ready, i + 1)
                        sp.dma_start(x1_v[:, ds(i * (PT * D), PT * D)],
                                     x1[:, :, :].rearrange("p t c -> p (t c)")).then_inc(x1_stored, 16)
                    sp.wait_ge(x1_stored, 16 * PIECES)

                @block.tensor
                def _(pe):
                    with pe.Fori(0, PIECES) as i:
                        for s in range(S):
                            k = i * S + s
                            pe.wait_ge(x_loaded[s], i * 16 + 16)
                            pe.wait_ge(xT_ready, i * S + max(s - 1, 0))
                            carry_wait(pe)
                            for t in range(CT):
                                last = nc.tensor.transpose(PS[0:D, s % 2, t * NP:(t + 1) * NP],
                                                           x_ring[:, s, t, :], ident[0:NP, 0:NP])
                            last.then_inc(x_turned[s], 1)
                            pe.wait_ge(xT_ready, k + 1)
                            pe.wait_ge(h2_ready, i * S + max(s - 1, 0))
                            nc.tensor.matmul(PS[0:D, 2 + s % 2, 0:CN].rearrange("f (t p) -> f t p", t=CT),
                                             W2_sb[:, :], table_t[:, ds(k * CT, CT), :],
                                             start=True, stop=True).then_inc(h2_put, 1)
                    with pe.Fori(0, PIECES) as i:
                        pe.wait_ge(z_ready, i)
                        for s in range(S):
                            pe.wait_ge(act_ready[s], i + 1)
                            carry_wait(pe)
                            for t in range(CT):
                                n = s * CT + t
                                last = nc.tensor.transpose(banks(0, 3, NP, PT * D)[:, n * D:(n + 1) * D],
                                                           act_ring[:, s, t * NP:(t + 1) * NP], ident[0:D, 0:D])
                            last.then_inc(act_turned[s], 1)
                        pe.wait_ge(x1_ready, i + 1)
                        pe.wait_ge(x1T_ready, i * S)
                        carry_wait(pe)
                        for s in range(S):
                            for t in range(CT):
                                last = nc.tensor.transpose(PS[0:D, 3 + s, t * NP:(t + 1) * NP],
                                                           x1[:, s * CT + t, :], ident[0:NP, 0:NP])
                        last.then_inc(x1_turned, 1)

                @block.scalar
                def _(act):
                    act.wait_ge(counts_done, 1)
                    with act.Fori(0, PIECES) as i:
                        for s in range(S):
                            k = i * S + s
                            here_t = table_t[0:D, ds(k * CT, CT), :]
                            act.wait_ge(x_turned[s], i + 1)
                            carry_wait(act)
                            act.activation(here_t, PS[0:D, s % 2, 0:CN].rearrange("f (t p) -> f t p", t=CT),
                                           ACT.Copy).then_inc(xT_ready, 1)
                            act.wait_ge(h2_put, k + 1)
                            carry_wait(act)
                            act.activation(here_t, PS[0:D, 2 + s % 2, 0:CN].rearrange("f (t p) -> f t p", t=CT),
                                           ACT.Identity, bias=b2c[:, :]).then_inc(h2_ready, 1)
                    act.wait_ge(var2_in, 1)
                    act.activation(root[:, :], moments[:, 1:2], ACT.Sqrt, bias=epsP[0:D, :]).then_inc(root2, 1)
                    act.wait_ge(bn2_ready, 1)
                    with act.Fori(0, PIECES) as i:
                        for s in range(S):
                            act.wait_ge(act_turned[s], i)
                            carry_wait(act)
                            act.activation(act_ring[:, s, :].rearrange("f (t p) -> f t p", t=CT),
                                           table_t[0:D, ds((i * S + s) * CT, CT), :], ACT.Silu,
                                           bias=shift2[:, :], scale=scale2[:, :]).then_inc(act_ready[s], 1)
                        act.wait_ge(ln_in, i + 1)
                        act.activation(small[:, 2, :], small[:, 1, :], ACT.Sqrt, bias=epsP[0:NP, :],
                                       scale=1.0 / D).then_inc(ln_root, 1)
                        act.wait_ge(x1_ready, i + 1)
                        carry_wait(act)
                        act.activation(x3[:, ds(i * PT, PT), :], x1[:, :, :], ACT.Copy).then_inc(x1_kept, 1)
                        act.wait_ge(x1_turned, i + 1)
                        carry_wait(act)
                        for s in range(S):
                            act.activation(table_t[0:D, ds((i * S + s) * CT, CT), :],
                                           PS[0:D, 3 + s, 0:CN].rearrange("f (t p) -> f t p", t=CT),
                                           ACT.Identity, scale=eps1c[:, :]).then_inc(x1T_ready, 1)

                @block.vector
                def _(dve):
                    chain = Chain(dve, count_chain)
                    quarter = NODES // 4
                    for n in range(4):
                        c, m = table[0:D, n * quarter:(n + 1) * quarter], table[D:P, n * quarter:(n + 1) * quarter]
                        chain.link(nc.vector.tensor_scalar(c, c, 1.0, None, ALU.max))
                        chain.link(nc.vector.reciprocal(counts[D:P, :], c))
                        chain.link(nc.vector.tensor_tensor(m, m, counts[D:P, :], ALU.mult))
                    nc.vector.tensor_scalar(eps1c[:, :], eps_c[:, :], 1.0, None, ALU.add).then_inc(counts_done, 1)
                    with dve.Fori(0, PIECES) as i:
                        for s in range(S):
                            k = i * S + s
                            dve.wait_ge(h2_ready, k + 1)
                            nc.vector.bn_stats(stats[:, ds(k * 6, 6)], table_t[0:D, ds(k * CT, CT), :]
                                               ).then_inc(h2_stats, 1)
                    dve.wait_ge(h2_stats, CHUNKS)
                    nc.vector.bn_aggr(moments[:, :], stats[:, :]).then_inc(var2_in, 1)
                    dve.wait_ge(root2, 1)
                    chain = Chain(dve, n_chain)
                    chain.link(nc.vector.reciprocal(root[:, :], root[:, :]))
                    chain.link(nc.vector.tensor_tensor(scale2[:, :], root[:, :], g2c[:, :], ALU.mult))
                    chain.link(nc.vector.tensor_tensor(root[:, :], moments[:, 0:1], scale2[:, :], ALU.mult))
                    nc.vector.tensor_tensor(shift2[:, :], be2c[:, :], root[:, :], ALU.subtract).then_inc(bn2_ready, 1)
                    with dve.Fori(0, PIECES) as i:
                        dve.wait_ge(act_turned[S - 1], i + 1)
                        dve.wait_ge(x1_ready, i)
                        nc.vector.tensor_tensor(z[:, :, :], x3[:, ds(i * PT, PT), :],
                                                banks(0, 3, NP, PT * D).rearrange("p (t c) -> p t c", c=D),
                                                ALU.add).then_inc(z_ready, 1)
                        dve.wait_ge(z_ready, i + 1)
                        dve.wait_ge(x1_kept, i)
                        dve.wait_ge(x1_turned, i)
                        dve.wait_ge(x1_stored, i * 16)
                        layer_norm(Chain(dve, ln_chain, i * LN_LINKS), z[:, :, :], sq[:, :, :], small,
                                   x1[:, :, :], ln_in, ln_root, i).then_inc(x1_ready, 1)

        clear_semaphores()

        with ExitStack() as here:
            E = sb(here, "E", [P, S, TG, D])
            X = sb(here, "X", [P, S, TG, D])
            msg = sb(here, "msg_c", [P, S, TG, D])
            hot = sb(here, "hot_c", [P, S, TG, WIN])
            e_loaded = sems("c_e_loaded")
            gathered = gathered_x1
            sum_ready = sems("sum_ready")
            idx_ready = sems("c_idx_ready")
            hot_ready = sems("c_hot_ready")
            msg_ready = sems("c_msg_ready")
            summed = sems("c_summed")
            added = sem("c_added")
            idx_first = sem("idx_first")

            with nc.Block() as block:
                @block.sync
                def _(sp):
                    with sp.Fori(0, SB) as i:
                        for s in range(S):
                            sp.wait_ge(msg_ready[s], i)
                            sp.dma_start(E[:, s, :, :], edge_v[i * S + s]).then_inc(e_loaded[s], 16)

                @block.gpsimd
                def _(pool):
                    pool.wait_ge(idx_first, 1)
                    with pool.Fori(0, SB) as i:
                        for s in range(S):
                            pool.wait_ge(idx_ready[s], i)
                            pool.wait_ge(sum_ready[s], i)
                            carry_wait(pool)
                            for j in range(TG):
                                nc.gpsimd.indirect_dma_start(
                                    out=X[:, s, j, :], out_offset=None, in_=x1_dram,
                                    in_offset=bass.IndirectOffsetOnAxis(ap=idx_ring[:, s, j:j + 1], axis=0)
                                ).then_inc(gathered[s], 16)

                @block.scalar
                def _(act):
                    with act.Fori(0, SB) as i:
                        for s in range(S):
                            act.wait_ge(sum_ready[s], i + 1)
                            act.wait_ge(summed[s], i)
                            act.activation(msg[:, s, :, :], E[:, s, :, :], ACT.Relu).then_inc(msg_ready[s], 1)

                @block.tensor
                def _(pe):
                    with pe.Fori(0, SB) as i:
                        for s in range(S):
                            pe.wait_ge(msg_ready[s], i + 1)
                            pe.wait_ge(hot_ready[s], i + 1)
                            pe.wait_ge(added, i * S + max(s - 1, 0))
                            for j in range(TG):
                                last = nc.tensor.matmul(PS[0:D, s % 2, 0:WIN], msg[:, s, j, :], hot[:, s, j, :],
                                                        start=(j == 0), stop=(j == TG - 1))
                            last.then_inc(summed[s], 1)

                @block.vector
                def _(dve):
                    nc.vector.tensor_copy(idx_flat, src_idx[:, 0:S * TG]).then_inc(idx_first, 1)
                    with dve.Fori(0, SB) as i:
                        for s in range(S):
                            g = i * S + s
                            first = dve.value_load(base_row[0:1, ds(g, 1)], min_val=0, max_val=NODES - 1)
                            dve.wait_ge(summed[s], i)
                            nc.vector.tensor_tensor(
                                hot[:, s, :, :], window[:, :].unsqueeze(1).to_broadcast([P, TG, WIN]),
                                rel5[:, ds(g, 1), :].rearrange("p a t -> p (a t)").unsqueeze(2)
                                .to_broadcast([P, TG, WIN]), ALU.is_equal).then_inc(hot_ready[s], 1)
                            dve.wait_ge(e_loaded[s], i * 16 + 16)
                            dve.wait_ge(gathered[s], i * (16 * TG) + 16 * TG)
                            nc.vector.tensor_tensor(E[:, s, :, :], X[:, s, :, :], E[:, s, :, :],
                                                    ALU.add).then_inc(sum_ready[s], 1)
                            nc.vector.tensor_copy(idx_ring[:, s, :],
                                                  src_idx[:, ds(i * (S * TG) + (S + s) * TG, TG)]
                                                  ).then_inc(idx_ready[s], 1)
                            dve.wait_ge(summed[s], i + 1)
                            dve.wait_ge(added, g)
                            nc.vector.tensor_tensor(table[0:D, ds(first, WIN)], table[0:D, ds(first, WIN)],
                                                    PS[0:D, s % 2, 0:WIN], ALU.add).then_inc(added, 1)

        with ExitStack() as here:
            E = sb(here, "E_g", [P, TG, D])
            X = sb(here, "X_g", [P, TG, D])
            msg = sb(here, "msg_h", [P, TG, D])
            hot = sb(here, "hot_h", [P, TG, WIN])
            cur = sb(here, "cur_h", [P, 2, TG])
            e_in = sem("gc_e_in")
            idx_in = sem("gc_idx_in")
            rows_in = gathered_general
            sum_in = sem("gc_sum_in")
            msg_ready = sem("gc_msg_ready")
            hot_ready = sem("gc_hot_ready")
            summed = sem("gc_summed")
            added = sem("gc_added")
            moved_on = sem("gc_moved_on")
            gc_chain = sem("gc_chain")
            with nc.Block() as block:
                @block.sync
                def _(sp):
                    with sp.If(sp.value_load(flag[0:1, 0:1], min_val=0, max_val=1) > 0):
                        with sp.Fori(0, G) as g:
                            sp.wait_ge(msg_ready, g)
                            sp.dma_start(E[:, :, :], edge_v[g]).then_inc(e_in, 16)

                @block.gpsimd
                def _(pool):
                    with pool.If(pool.value_load(flag[0:1, 0:1], min_val=0, max_val=1) > 0):
                        with pool.Fori(0, G) as g:
                            pool.wait_ge(idx_in, g + 1)
                            carry_wait(pool)
                            for j in range(TG):
                                nc.gpsimd.indirect_dma_start(
                                    out=X[:, j, :], out_offset=None, in_=x1_dram,
                                    in_offset=bass.IndirectOffsetOnAxis(ap=idx_ring[:, 0, j:j + 1], axis=0)
                                ).then_inc(rows_in, 16)

                @block.scalar
                def _(act):
                    with act.If(act.value_load(flag[0:1, 0:1], min_val=0, max_val=1) > 0):
                        with act.Fori(0, G) as g:
                            act.wait_ge(sum_in, g + 1)
                            act.wait_ge(added, g * NW)
                            act.activation(msg[:, :, :], E[:, :, :], ACT.Relu).then_inc(msg_ready, 1)

                @block.tensor
                def _(pe):
                    with pe.If(pe.value_load(flag[0:1, 0:1], min_val=0, max_val=1) > 0):
                        with pe.Fori(0, G) as g:
                            pe.wait_ge(msg_ready, g + 1)
                            carry_wait(pe)
                            with pe.Fori(0, NW) as w:
                                pe.wait_ge(hot_ready, g * NW + w + 1)
                                pe.wait_ge(added, g * NW + w)
                                for j in range(TG):
                                    last = nc.tensor.matmul(PS[0:D, 1, 0:WIN], msg[:, j, :], hot[:, j, :],
                                                            start=(j == 0), stop=(j == TG - 1))
                                last.then_inc(summed, 1)

                @block.vector
                def _(dve):
                    with dve.If(dve.value_load(flag[0:1, 0:1], min_val=0, max_val=1) > 0):
                        with dve.Fori(0, G) as g:
                            nc.vector.tensor_copy(idx_ring[:, 0, :], src_idx[:, ds(g * TG, TG)]).then_inc(idx_in, 1)
                            dve.wait_ge(e_in, g * 16 + 16)
                            dve.wait_ge(rows_in, g * (16 * TG) + 16 * TG)
                            nc.vector.tensor_tensor(E[:, :, :], X[:, :, :], E[:, :, :], ALU.add).then_inc(sum_in, 1)
                            chain = Chain(dve, gc_chain, g * 6)
                            dve.wait_ge(moved_on, g * NW)
                            outside(dve, chain, cur, rel5[:, ds(g, 1), :].rearrange("p a t -> p (a t)"),
                                    base_all[:, ds(g, 1)], P)
                            carry_wait(dve)
                            with dve.Fori(0, NW) as w:
                                dve.wait_ge(summed, g * NW + w)
                                dve.wait_ge(moved_on, g * NW + w)
                                nc.vector.tensor_tensor(
                                    hot[:, :, :], window[:, :].unsqueeze(1).to_broadcast([P, TG, WIN]),
                                    cur[:, 0, :].unsqueeze(2).to_broadcast([P, TG, WIN]),
                                    ALU.is_equal).then_inc(hot_ready, 1)
                                dve.wait_ge(hot_ready, g * NW + w + 1)
                                nc.vector.tensor_scalar(cur[:, 0, :], cur[:, 0, :], -float(WIN), None,
                                                        ALU.add).then_inc(moved_on, 1)
                                dve.wait_ge(summed, g * NW + w + 1)
                                dve.wait_ge(added, g * NW + w)
                                nc.vector.tensor_tensor(table[0:D, ds(w * WIN, WIN)], table[0:D, ds(w * WIN, WIN)],
                                                        PS[0:D, 1, 0:WIN], ALU.add).then_inc(added, 1)

        clear_semaphores()

        with ExitStack() as here:
            act_ring = sb(here, "act_ring_o", [D, S, CN])
            z = sb(here, "z_o", [NP, PT, D])
            sq = sb(here, "sq_o", [NP, PT, D])
            small = sb(here, "small_o", [NP, 3, PT])
            y = sb(here, "y", [NP, PT, D])
            lin_put = sems("lin_put")
            act_ready = sems("o_act_ready")
            act_turned = sems("o_act_turned")
            z_ready = sem("o_z_ready")
            ln_chain = sem("o_ln_chain")
            ln_in = sem("o_ln_in")
            ln_root = sem("o_ln_root")
            y_ready = sem("y_ready")
            y_stored = sem("y_stored")
            with nc.Block() as block:
                @block.sync
                def _(sp):
                    with sp.Fori(0, PIECES) as i:
                        sp.wait_ge(y_ready, i + 1)
                        sp.dma_start(out_v[:, ds(i * (PT * D), PT * D)],
                                     y[:, :, :].rearrange("p t c -> p (t c)")).then_inc(y_stored, 16)
                    sp.wait_ge(y_stored, 16 * PIECES)

                @block.tensor
                def _(pe):
                    with pe.Fori(0, PIECES) as i:
                        for s in range(S):
                            pe.wait_ge(act_ready[s], i)
                            nc.tensor.matmul(PS[:, 3 + s, 0:CN].rearrange("f (t p) -> f t p", t=CT), W3T[:, :],
                                             table_t[0:D, ds((i * S + s) * CT, CT), :],
                                             start=True, stop=True).then_inc(lin_put[s], 1)
                        pe.wait_ge(z_ready, i)
                        for s in range(S):
                            pe.wait_ge(act_ready[s], i + 1)
                            carry_wait(pe)
                            for t in range(CT):
                                n = s * CT + t
                                last = nc.tensor.transpose(banks(0, 3, NP, PT * D)[:, n * D:(n + 1) * D],
                                                           act_ring[:, s, t * NP:(t + 1) * NP], ident[0:D, 0:D])
                            last.then_inc(act_turned[s], 1)

                @block.scalar
                def _(act):
                    with act.Fori(0, PIECES) as i:
                        for s in range(S):
                            act.wait_ge(lin_put[s], i + 1)
                            act.wait_ge(act_turned[s], i)
                            act.activation(act_ring[:, s, :], PS[0:D, 3 + s, 0:CN], ACT.Relu,
                                           bias=b3c[:, :]).then_inc(act_ready[s], 1)
                        act.wait_ge(ln_in, i + 1)
                        act.activation(small[:, 2, :], small[:, 1, :], ACT.Sqrt, bias=epsP[0:NP, :],
                                       scale=1.0 / D).then_inc(ln_root, 1)

                @block.vector
                def _(dve):
                    with dve.Fori(0, PIECES) as i:
                        dve.wait_ge(act_turned[S - 1], i + 1)
                        dve.wait_ge(y_ready, i)
                        nc.vector.tensor_tensor(z[:, :, :], x3[:, ds(i * PT, PT), :],
                                                banks(0, 3, NP, PT * D).rearrange("p (t c) -> p t c", c=D),
                                                ALU.add).then_inc(z_ready, 1)
                        dve.wait_ge(z_ready, i + 1)
                        dve.wait_ge(y_stored, i * 16)
                        layer_norm(Chain(dve, ln_chain, i * LN_LINKS), z[:, :, :], sq[:, :, :], small,
                                   y[:, :, :], ln_in, ln_root, i).then_inc(y_ready, 1)


_INS = ['x', 'src', 'dst', 'edge_attr_64', 'L0_gnn_W1', 'L0_gnn_b1', 'L0_gnn_g1', 'L0_gnn_be1',
        'L0_gnn_W2', 'L0_gnn_b2', 'L0_gnn_g2', 'L0_gnn_be2', 'L1_gnn_W', 'L1_gnn_b', 'L1_gnn_eps']


def kernel(**inputs):
    import numpy as _np
    import concourse.bacc as _bacc
    from concourse import mybir as _mybir
    from concourse.bass_utils import run_bass_kernel_spmd as _run

    nc = _bacc.Bacc("TRN2", target_bir_lowering=False, num_devices=1)
    arrays, args = {}, []
    for name in _INS:
        a = _np.ascontiguousarray(inputs[name])
        if a.ndim == 0:
            a = a.reshape(1)
        arrays[f"in_{name}_dram"] = a
        args.append(nc.dram_tensor(f"in_{name}_dram", a.shape, _mybir.dt.from_np(a.dtype), kind="ExternalInput").ap())
    args.append(nc.dram_tensor("out_dram", inputs["x"].shape, _mybir.dt.float32, kind="ExternalOutput").ap())
    gnn_kernel(nc, *args)
    r = _run(nc, [arrays], core_ids=[0])
    return r.results[0]["out_dram"]
```

```python
import concourse.bass as bass
from concourse import mybir
from contextlib import ExitStack



class Chain:

    def __init__(self, engine, sem, base=0):
        self.engine, self.sem, self.base, self.n = engine, sem, base, 0

    def link(self, instruction):
        self.n += 1
        instruction.then_inc(self.sem, 1)
        self.engine.wait_ge(self.sem, self.base + self.n)


def reuse(engine, sem, n):
    if not (isinstance(n, int) and n == 0):
        engine.wait_ge(sem, n)


def gnn_kernel(nc, x, src, dst, edge, W1, b1, g1, be1, W2, b2, g2, be2, W3, b3, eps1, out):
    fp32 = mybir.dt.float32
    int32 = mybir.dt.int32
    bf16 = mybir.dt.bfloat16
    ALU = mybir.AluOpType
    ACT = mybir.ActivationFunctionType
    AX = mybir.AxisListType.X
    ds = bass.ds

    P = 128
    NODES, D = x.shape
    EDGES = edge.shape[0]
    EPS = 1e-5
    TG = 5
    EG = TG * P
    S = 5
    G = EDGES // EG
    SB = G // S
    WIN = 64
    NW = -(-NODES // WIN)
    HC = TG * D
    NP = 125
    NT = NODES // NP
    CT = 4
    CN = CT * NP
    PT = S * CT
    PIECES = NT // PT
    CHUNKS = NT // CT
    assert EDGES == G * EG and G == SB * S and SB <= P and NODES == NP * NT and NT == PIECES * PT

    edge_v = edge.rearrange("(g p j) c -> g p j c", p=P, j=TG)
    src_v = src.rearrange("(sb n) -> sb n", sb=SB)
    dst_v = dst.rearrange("(sb n) -> sb n", sb=SB)
    first_v = dst.rearrange("(o g n) -> o g n", o=1, n=EG)[:, :, 0]
    x_v = x.rearrange("(p t) c -> p t c", p=NP)
    out_v = out.rearrange("(p t) c -> p (t c)", p=NP)
    h_dram = nc.dram_tensor("h_scratch", (G, P, HC), fp32, kind="Internal").ap()
    x1_dram = nc.dram_tensor("x1_scratch", (NODES, D), fp32, kind="Internal").ap()
    x1_v = x1_dram.rearrange("(p t) c -> p (t c)", p=NP)

    def col(v):
        return v.rearrange("(a b) -> a b", b=1)

    ctx = ExitStack()
    with ctx:
        def sb(where, name, shape, dt=fp32):
            return where.enter_context(nc.sbuf_tensor(name, shape, dt))

        in_use = []

        def sem(name):
            in_use.append(nc.alloc_semaphore(name))
            return in_use[-1]

        def sems(name):
            return [sem(f"{name}{s}") for s in range(S)]

        def clear_semaphores():
            nc.clear_and_free_semaphores(list(in_use))
            nc.all_engine_barrier()
            in_use.clear()

        steps = ctx.enter_context(nc.semaphore("steps"))

        def carry_wait(engine):
            engine.sem_inc(steps, 1)

        gathered_x = [ctx.enter_context(nc.semaphore(f"gathered_x{s}")) for s in range(S)]
        gathered_x1 = [ctx.enter_context(nc.semaphore(f"gathered_x1{s}")) for s in range(S)]
        gathered_general = ctx.enter_context(nc.semaphore("gathered_general"))

        table = sb(ctx, "table", [P, NODES + WIN])
        x_nodes = sb(ctx, "x_nodes", [NP, NT * D])
        src_idx = sb(ctx, "src_idx", [P, (SB + 1) * S * TG], int32)
        rel5 = sb(ctx, "rel5", [P, G, TG])
        rel6 = sb(ctx, "rel6", [P, G, 6])
        base_all = sb(ctx, "base_all", [P, G])
        base_row = sb(ctx, "base_row", [1, G], int32)
        idx_ring = sb(ctx, "idx_ring", [P, S, TG], int32)
        ident = sb(ctx, "ident", [P, P])
        halves = sb(ctx, "halves", [P, P])
        window = sb(ctx, "window", [P, WIN])
        flag = sb(ctx, "flag", [1, 1], int32)
        W1_sb = sb(ctx, "W1_sb", [2 * D, D])
        W2_sb = sb(ctx, "W2_sb", [2 * D, D])
        W3T = sb(ctx, "W3T", [D, 2 * D])
        b1c = sb(ctx, "b1c", [P, 1])
        g1c = sb(ctx, "g1c", [P, 1])
        be1c = sb(ctx, "be1c", [P, 1])
        b2c = sb(ctx, "b2c", [D, 1])
        g2c = sb(ctx, "g2c", [D, 1])
        be2c = sb(ctx, "be2c", [D, 1])
        b3c = sb(ctx, "b3c", [D, 1])
        eps_c = sb(ctx, "eps_c", [D, 1])
        scale1 = sb(ctx, "scale1", [P, 1])
        shift1 = sb(ctx, "shift1", [P, 1])
        scale2 = sb(ctx, "scale2", [D, 1])
        shift2 = sb(ctx, "shift2", [D, 1])
        epsP = sb(ctx, "epsP", [P, 1])
        PS = ctx.enter_context(nc.psum_tensor("PS", [P, 8, 512], fp32))

        def banks(first, n, parts, cols):
            return PS[0:parts, first:first + n, :].rearrange("p b c -> p (b c)")[:, 0:cols]

        x3 = x_nodes[:, :].rearrange("p (t c) -> p t c", c=D)
        table_t = table[:, 0:NODES].rearrange("f (p t) -> f t p", t=NT)
        idx_flat = idx_ring[:, :, :].rearrange("p s j -> p (s j)")

        with ExitStack() as here:
            src_rows = sb(here, "src_rows", [SB, S * EG], int32)
            dst_rows = sb(here, "dst_rows", [SB, S * EG], int32)
            iota_i = sb(here, "iota_i", [P, WIN], int32)
            base_f = sb(here, "base_f", [1, G])
            ones_row = sb(here, "ones_row", [1, P])
            ones_col = sb(here, "ones_col", [P, 1])
            W3_sb = sb(here, "W3_sb", [D, D])
            most = sb(here, "most", [P, 1])
            least = sb(here, "least", [P, 1])
            bad = sb(here, "bad", [P, 1])
            flag_f = sb(here, "flag_f", [1, 1])
            src_f = src_rows[:, :].bitcast(fp32)
            dst_f = dst_rows[:, :].bitcast(fp32)
            srcT = src_f.rearrange("sb (q p j) -> sb q j p", q=S, j=TG)
            dstT = dst_f.rearrange("sb (q p j) -> sb q j p", q=S, j=TG)

            s_src = sem("s_src")
            s_dst = sem("s_dst")
            s_first = sem("s_first")
            s_x = sem("s_x")
            s_w = sem("s_w")
            s_zero = sem("s_zero")
            s_ident = sem("s_ident")
            s_iota = sem("s_iota")
            s_const = sem("s_const")
            src_float = sem("src_float")
            dst_float = sem("dst_float")
            first_float = sem("first_float")
            pieces_put = sem("pieces_put")
            pieces_taken = sem("pieces_taken")
            base_put = sem("base_put")
            w3_put = sem("w3_put")
            bad_ready = sem("bad_ready")
            bad_sum = sem("bad_sum")
            prep_chain = sem("prep_chain")

            with nc.Block() as block:
                @block.sync
                def _(sp):
                    sp.dma_start(src_rows[:, :], src_v).then_inc(s_src, 16)
                    sp.dma_start(dst_rows[:, :], dst_v).then_inc(s_dst, 16)
                    sp.dma_start(base_row[:, :], first_v, allow_slow_non_contiguous=True).then_inc(s_first, 16)
                    sp.dma_start(x_nodes[:, :], x_v.rearrange("p t c -> p (t c)")).then_inc(s_x, 16)
                    sp.wait_ge(s_x, 16)

                @block.scalar
                def _(act):
                    for to, of in ((W3_sb[:, :], W3), (W1_sb[:, :], W1), (W2_sb[:, :], W2),
                                   (b1c[0:D, :], col(b1)), (b1c[D:P, :], col(b1)),
                                   (g1c[0:D, :], col(g1)), (g1c[D:P, :], col(g1)),
                                   (be1c[0:D, :], col(be1)), (be1c[D:P, :], col(be1)),
                                   (b2c[:, :], col(b2)), (g2c[:, :], col(g2)), (be2c[:, :], col(be2)),
                                   (b3c[:, :], col(b3)), (eps_c[:, :], eps1.partition_broadcast(D))):
                        act.dma_start(to, of).then_inc(s_w, 16)
                    act.wait_ge(s_w, 16 * 14)

                @block.gpsimd
                def _(pool):
                    nc.gpsimd.memset(ident[:, :], 0.0).then_inc(s_zero, 1)
                    pool.wait_ge(s_zero, 1)
                    nc.gpsimd.affine_select(out=ident[:, :], in_=ident[:, :], compare_op=ALU.not_equal,
                                            fill=1.0, base=0, pattern=[[-1, P]],
                                            channel_multiplier=1).then_inc(s_ident, 1)
                    nc.gpsimd.memset(ones_row[:, :], 1.0)
                    nc.gpsimd.memset(ones_col[:, :], 1.0)
                    nc.gpsimd.memset(epsP[:, :], EPS)
                    nc.gpsimd.memset(src_idx[:, G * TG:], 0).then_inc(s_const, 1)
                    nc.gpsimd.iota(iota_i[:, :], pattern=[[1, WIN]], base=0,
                                   channel_multiplier=0).then_inc(s_iota, 1)
                    pool.wait_ge(s_iota, 1)
                    nc.gpsimd.tensor_copy(window[:, :], iota_i[:, :]).then_inc(s_const, 1)

                @block.tensor
                def _(pe):
                    pe.wait_ge(s_ident, 1)
                    for n in range(2 * S):
                        rows, q = (srcT, n) if n < S else (dstT, n - S)
                        if n == 0:
                            pe.wait_ge(src_float, 1)
                        if n == S:
                            pe.wait_ge(dst_float, 1)
                        if n >= 2:
                            pe.wait_ge(pieces_taken, n - 1)
                        for j in range(TG):
                            to = banks(2 * (n % 2), 2, P, TG * P)[:, j * P:j * P + SB]
                            last = nc.tensor.transpose(to, rows[:, q, j, :], ident[0:SB, 0:SB])
                        last.then_inc(pieces_put, 1)
                    pe.wait_ge(first_float, 1)
                    pe.wait_ge(s_const, 1)
                    for c in range(0, G, 512):
                        n = min(512, G - c)
                        last = nc.tensor.matmul(PS[:, 4 + c // 512, 0:n], ones_row[:, :],
                                                base_f[0:1, c:c + n], start=True, stop=True)
                    last.then_inc(base_put, 1)
                    pe.wait_ge(s_w, 16 * 14)
                    nc.tensor.transpose(PS[0:D, 6, 0:D], W3_sb[:, :], ident[0:D, 0:D]).then_inc(w3_put, 1)
                    pe.wait_ge(bad_ready, 1)
                    nc.tensor.matmul(PS[0:1, 7, 0:1], bad[:, :], ones_col[:, :], start=True,
                                     stop=True).then_inc(bad_sum, 1)

                @block.vector
                def _(dve):
                    chain = Chain(dve, prep_chain)
                    nc.vector.memset(rel6[D:P, :, 4:6], -1.0)
                    dve.wait_ge(s_src, 16)
                    nc.vector.tensor_copy(src_f, src_rows[:, :]).then_inc(src_float, 1)
                    dve.wait_ge(s_dst, 16)
                    nc.vector.tensor_copy(dst_f, dst_rows[:, :]).then_inc(dst_float, 1)
                    dve.wait_ge(s_first, 16)
                    nc.vector.tensor_copy(base_f[:, :], base_row[:, :]).then_inc(first_float, 1)
                    dve.wait_ge(s_const, 1)
                    for n in range(2 * S):
                        to, q = (src_idx[:, 0:G * TG], n) if n < S else \
                            (rel5[:, :, :].rearrange("p g j -> p (g j)"), n - S)
                        dve.wait_ge(pieces_put, n + 1)
                        put = banks(2 * (n % 2), 2, P, TG * P).rearrange("p (j c) -> p j c", j=TG)
                        last = nc.vector.tensor_copy(
                            to.rearrange("p (sb q j) -> p q j sb", q=S, j=TG)[:, q, :, :], put[:, :, 0:SB])
                        last.then_inc(pieces_taken, 1)
                    dve.wait_ge(pieces_taken, 2 * S)
                    chain.link(nc.vector.tensor_copy(idx_flat, src_idx[:, 0:S * TG]))
                    dve.wait_ge(base_put, 1)
                    chain.link(nc.vector.tensor_copy(base_all[:, :], banks(4, 2, P, G)))
                    chain.link(nc.vector.tensor_tensor(
                        rel5[:, :, :], rel5[:, :, :],
                        base_all[:, :].unsqueeze(2).to_broadcast([P, G, TG]), ALU.subtract))
                    nc.vector.tensor_copy(rel6[:, :, 0:2], rel5[:, :, 0:4:2])
                    nc.vector.tensor_copy(rel6[:, :, 2:4], rel5[:, :, 1:4:2])
                    nc.vector.tensor_copy(rel6[0:D, :, 4:5], rel5[0:D, :, 4:5])
                    nc.vector.tensor_copy(rel6[0:D, :, 5:6], rel5[D:P, :, 4:5])
                    rel_flat = rel5[:, :, :].rearrange("p g j -> p (g j)")
                    nc.vector.reduce_max(most[:, :], rel_flat, AX)
                    chain.link(nc.vector.tensor_reduce(least[:, :], rel_flat, AX, ALU.min))
                    chain.link(nc.vector.tensor_scalar(most[:, :], most[:, :], float(WIN - 1), None, ALU.is_gt))
                    chain.link(nc.vector.tensor_scalar(least[:, :], least[:, :], 0.0, None, ALU.is_lt))
                    nc.vector.tensor_tensor(bad[:, :], most[:, :], least[:, :], ALU.add).then_inc(bad_ready, 1)
                    dve.wait_ge(bad_sum, 1)
                    chain.link(nc.vector.tensor_scalar(flag_f[:, :], PS[0:1, 7, 0:1], 0.0, None, ALU.is_gt))
                    nc.vector.tensor_copy(flag[:, :], flag_f[:, :])
                    dve.wait_ge(w3_put, 1)
                    for c in (0, D):
                        nc.vector.tensor_copy(W3T[:, c:c + D], PS[0:D, 6, 0:D])
                    for c in (0, D):
                        last = nc.vector.tensor_tensor(halves[:, c:c + D], ident[:, 0:D], ident[:, D:P], ALU.add)
                    chain.link(last)
                    nc.vector.tensor_scalar(halves[:, :], halves[:, :], 0.5, None, ALU.mult)
                    nc.vector.memset(table[:, :], 0.0)

        with ExitStack() as here:
            Z = sb(here, "Z", [P, S, TG, 2 * D])
            ZT = sb(here, "ZT", [P, EG])
            h_ring = sb(here, "h_ring", [P, S, HC])
            stats = sb(here, "stats", [P, G * 6])
            moments = sb(here, "moments", [P, 2])
            mean = sb(here, "mean", [P, 1])
            off = sb(here, "off", [P, 1])
            var = sb(here, "var", [P, 1])
            ones_bf = sb(here, "ones_bf", [P, D], bf16)
            hot = sb(here, "hot_a", [P, S, TG, WIN], bf16)

            ones_ready = sem("ones_ready")
            hot_ready = sems("a_hot_ready")
            counted = sems("counted")
            count_added = sem("count_added")
            e_loaded = sems("e_loaded")
            gathered = gathered_x
            rows_done = sems("rows_done")
            zt_taken = sem("zt_taken")
            h_put = sem("h_put")
            h_ready = sems("h_ready")
            h_stored = sems("h_stored")
            stats_done = sems("stats_done")
            idx_ready = sems("idx_ready")
            mean_in = sem("mean_in")
            mean_put = sem("mean_put")
            var_in = sem("var_in")
            var_put = sem("var_put")
            var_sb = sem("var_sb")
            root1 = sem("root1")
            a_chain = sem("a_chain")

            with nc.Block() as block:
                @block.sync
                def _(sp):
                    def turn(i):
                        for s in range(S):
                            reuse(sp, rows_done[s], i)
                            sp.dma_start(Z[:, s, :, D:2 * D], edge_v[i * S + s]).then_inc(e_loaded[s], 16)

                    turn(0)
                    with sp.Fori(1, SB) as i:
                        turn(i)

                @block.gpsimd
                def _(pool):
                    def turn(i):
                        for s in range(S):
                            reuse(pool, idx_ready[s], i)
                            reuse(pool, rows_done[s], i)
                            carry_wait(pool)
                            for j in range(TG):
                                nc.gpsimd.indirect_dma_start(
                                    out=Z[:, s, j, 0:D], out_offset=None, in_=x,
                                    in_offset=bass.IndirectOffsetOnAxis(ap=idx_ring[:, s, j:j + 1], axis=0)
                                ).then_inc(gathered[s], 16)

                    turn(0)
                    with pool.Fori(1, SB) as i:
                        turn(i)

                @block.tensor
                def _(pe):
                    pe.wait_ge(ones_ready, 1)

                    def turn(i):
                        for s in range(S):
                            g = i * S + s
                            rows_at = 2 * (s % 2)
                            reuse(pe, zt_taken, i * S if s < 2 else g - 1)
                            pe.wait_ge(e_loaded[s], i * 16 + 16)
                            pe.wait_ge(gathered[s], i * (16 * TG) + 16 * TG)
                            for j in range(TG):
                                last = nc.tensor.transpose(banks(rows_at, 2, P, EG)[:, j * P:(j + 1) * P],
                                                           Z[:, s, j, :], ident[:, :])
                            last.then_inc(rows_done[s], 1)
                            pe.wait_ge(zt_taken, g + 1)
                            h = PS[:, 4 + s % 2, 0:HC]
                            for half in (0, 1):
                                lo = half * D
                                nc.tensor.matmul(h[lo:lo + D, 0:2 * P], W1_sb[:, :],
                                                 ZT[:, half * 2 * P:(half + 1) * 2 * P], start=True, stop=True)
                                last = nc.tensor.matmul(h[lo:lo + D, 2 * P:HC], W1_sb[:, :],
                                                        ZT[:, 4 * P + lo:4 * P + lo + D], start=True, stop=True)
                            last.then_inc(h_put, 1)
                            pe.wait_ge(hot_ready[s], i + 1)
                            reuse(pe, count_added, i * S + max(s - 1, 0))
                            for j in range(TG):
                                last = nc.tensor.matmul(PS[0:D, 6 + s % 2, 0:WIN], ones_bf[:, :], hot[:, s, j, :],
                                                        start=(j == 0), stop=(j == TG - 1))
                            last.then_inc(counted[s], 1)

                    turn(0)
                    with pe.Fori(1, SB) as i:
                        turn(i)
                    pe.wait_ge(count_added, G)
                    pe.wait_ge(mean_in, 1)
                    nc.tensor.matmul(PS[:, 6, 0:1], halves[:, :], moments[:, 0:1], start=True,
                                     stop=True).then_inc(mean_put, 1)
                    pe.wait_ge(var_in, 1)
                    nc.tensor.matmul(PS[:, 7, 0:1], halves[:, :], var[:, :], start=True,
                                     stop=True).then_inc(var_put, 1)

                @block.scalar
                def _(act):
                    def turn(i):
                        for s in range(S):
                            g = i * S + s
                            act.wait_ge(rows_done[s], i + 1)
                            act.activation(ZT[:, :], banks(2 * (s % 2), 2, P, EG), ACT.Copy).then_inc(zt_taken, 1)
                            act.wait_ge(h_put, g + 1)
                            reuse(act, h_stored[s], i * 16)
                            reuse(act, stats_done[s], i)
                            act.activation(h_ring[:, s, :], PS[:, 4 + s % 2, 0:HC], ACT.Identity,
                                           bias=b1c[:, :]).then_inc(h_ready[s], 1)
                            act.wait_ge(h_ready[s], i + 1)
                            act.dma_start(h_dram[g], h_ring[:, s, :]).then_inc(h_stored[s], 16)

                    turn(0)
                    with act.Fori(1, SB) as i:
                        turn(i)
                    act.wait_ge(var_sb, 1)
                    act.activation(var[:, :], var[:, :], ACT.Sqrt, bias=epsP[:, :]).then_inc(root1, 1)
                    for s in range(S):
                        act.wait_ge(h_stored[s], 16 * SB)

                @block.vector
                def _(dve):
                    nc.vector.memset(ones_bf[:, :], 1.0).then_inc(ones_ready, 1)

                    def turn(i):
                        for s in range(S):
                            g = i * S + s
                            first = dve.value_load(base_row[0:1, ds(g, 1)], min_val=0, max_val=NODES - 1)
                            reuse(dve, counted[s], i)
                            nc.vector.tensor_tensor(
                                hot[:, s, :, :], window[:, :].unsqueeze(1).to_broadcast([P, TG, WIN]),
                                rel5[:, ds(g, 1), :].rearrange("p a t -> p (a t)").unsqueeze(2)
                                .to_broadcast([P, TG, WIN]), ALU.is_equal).then_inc(hot_ready[s], 1)
                            dve.wait_ge(h_ready[s], i + 1)
                            nc.vector.bn_stats(stats[:, ds(i * (6 * S) + 6 * s, 6)],
                                               h_ring[:, s, :]).then_inc(stats_done[s], 1)
                            nc.vector.tensor_copy(idx_ring[:, s, :],
                                                  src_idx[:, ds(i * (S * TG) + (S + s) * TG, TG)]
                                                  ).then_inc(idx_ready[s], 1)
                            dve.wait_ge(counted[s], i + 1)
                            reuse(dve, count_added, i * S + s)
                            nc.vector.tensor_tensor(table[0:D, ds(first, WIN)], table[0:D, ds(first, WIN)],
                                                    PS[0:D, 6 + s % 2, 0:WIN], ALU.add).then_inc(count_added, 1)

                    turn(0)
                    with dve.Fori(1, SB) as i:
                        turn(i)
                    chain = Chain(dve, a_chain)
                    dve.wait_ge(stats_done[S - 1], SB)
                    nc.vector.bn_aggr(moments[:, :], stats[:, :]).then_inc(mean_in, 1)
                    dve.wait_ge(mean_put, 1)
                    chain.link(nc.vector.tensor_copy(mean[:, :], PS[:, 6, 0:1]))
                    chain.link(nc.vector.tensor_tensor(off[:, :], moments[:, 0:1], mean[:, :], ALU.subtract))
                    chain.link(nc.vector.tensor_tensor(off[:, :], off[:, :], off[:, :], ALU.mult))
                    nc.vector.tensor_tensor(var[:, :], moments[:, 1:2], off[:, :], ALU.add).then_inc(var_in, 1)
                    dve.wait_ge(var_put, 1)
                    nc.vector.tensor_copy(var[:, :], PS[:, 7, 0:1]).then_inc(var_sb, 1)
                    dve.wait_ge(root1, 1)
                    chain.link(nc.vector.reciprocal(scale1[:, :], var[:, :]))
                    chain.link(nc.vector.tensor_tensor(scale1[:, :], scale1[:, :], g1c[:, :], ALU.mult))
                    chain.link(nc.vector.tensor_tensor(off[:, :], mean[:, :], scale1[:, :], ALU.mult))
                    nc.vector.tensor_tensor(shift1[:, :], be1c[:, :], off[:, :], ALU.subtract)

        clear_semaphores()

        def pass_b(here):
            h_ring = sb(here, "hb_ring", [P, S, HC])
            m_ring = sb(here, "m_ring", [P, S, HC])
            msg = sb(here, "msg", [P, S, 6, D])
            hot = sb(here, "hot", [P, S, 6, WIN])

            h_loaded = sems("h_loaded")
            silu_done = sems("silu_done")
            turned = sems("turned")
            msg_ready = sems("msg_ready")
            hot_ready = sems("hot_ready")
            summed = sems("summed")
            added = sem("added")
            b_const = sem("b_const")

            def bank_t(s):
                return s % 3

            def bank_o(s):
                return 3 + s % 3

            with nc.Block() as block:
                @block.sync
                def _(sp):
                    def turn(i):
                        for s in range(S):
                            reuse(sp, silu_done[s], i)
                            sp.dma_start(h_ring[:, s, :], h_dram[i * S + s]).then_inc(h_loaded[s], 16)

                    turn(0)
                    with sp.Fori(1, SB) as i:
                        turn(i)

                @block.scalar
                def _(act):
                    def silu(i, s):
                        act.wait_ge(h_loaded[s], i * 16 + 16)
                        reuse(act, turned[s], i)
                        act.activation(m_ring[:, s, :], h_ring[:, s, :], ACT.Silu, bias=shift1[:, :],
                                       scale=scale1[:, :]).then_inc(silu_done[s], 1)

                    def take(i, s):
                        act.wait_ge(turned[s], i + 1)
                        reuse(act, summed[s], i)
                        act.activation(msg[:, s, :, :],
                                       PS[:, bank_t(s), 0:6 * D].rearrange("p (t c) -> p t c", c=D),
                                       ACT.Copy).then_inc(msg_ready[s], 1)

                    act.wait_ge(b_const, 1)
                    silu(0, 0)
                    for s in range(S):
                        silu((s + 1) // S, (s + 1) % S)
                        take(0, s)
                    with act.Fori(1, SB - 1) as i:
                        for s in range(S):
                            silu(i + (s + 1) // S, (s + 1) % S)
                            take(i, s)
                    for s in range(S):
                        if s + 1 < S:
                            silu(SB - 1, s + 1)
                        take(SB - 1, s)

                @block.tensor
                def _(pe):
                    def turn(i, s):
                        pe.wait_ge(silu_done[s], i + 1)
                        if s >= 3:
                            pe.wait_ge(msg_ready[s - 3], i + 1)
                        else:
                            reuse(pe, msg_ready[s + 3 if s < 2 else s], i)
                        for c, (at, n) in enumerate(((0, P), (P, P), (2 * P, D))):
                            last = nc.tensor.transpose(PS[0:n, bank_t(s), c * P:(c + 1) * P],
                                                       m_ring[:, s, at:at + n], ident[:, :])
                        last.then_inc(turned[s], 1)

                    def products(i, s):
                        pe.wait_ge(msg_ready[s], i + 1)
                        pe.wait_ge(hot_ready[s], i + 1)
                        reuse(pe, added, i * S + max(s - 2, 0))
                        for t in range(6):
                            k = P if t < 4 else D
                            last = nc.tensor.matmul(PS[D:P, bank_o(s), 0:WIN], msg[0:k, s, t, :], hot[0:k, s, t, :],
                                                    start=(t == 0), stop=(t == 5))
                        last.then_inc(summed[s], 1)

                    pe.wait_ge(b_const, 1)
                    turn(0, 0)
                    for s in range(S):
                        turn((s + 1) // S, (s + 1) % S)
                        products(0, s)
                    with pe.Fori(1, SB - 1) as i:
                        for s in range(S):
                            turn(i + (s + 1) // S, (s + 1) % S)
                            products(i, s)
                    for s in range(S):
                        if s + 1 < S:
                            turn(SB - 1, s + 1)
                        products(SB - 1, s)

                @block.vector
                def _(dve):
                    def one_hot(i, s):
                        reuse(dve, summed[s], i)
                        nc.vector.tensor_tensor(
                            hot[:, s, :, :], window[:, :].unsqueeze(1).to_broadcast([P, 6, WIN]),
                            rel6[:, ds(i * S + s, 1), :].rearrange("p a t -> p (a t)").unsqueeze(2)
                            .to_broadcast([P, 6, WIN]), ALU.is_equal).then_inc(hot_ready[s], 1)

                    def add(i, s):
                        first = dve.value_load(base_row[0:1, ds(i * S + s, 1)], min_val=0, max_val=NODES - 1)
                        dve.wait_ge(summed[s], i + 1)
                        reuse(dve, added, i * S + s)
                        nc.vector.tensor_tensor(table[D:P, ds(first, WIN)], table[D:P, ds(first, WIN)],
                                                PS[D:P, bank_o(s), 0:WIN], ALU.add).then_inc(added, 1)

                    nc.vector.memset(PS[:, 0:3, :], 0.0).then_inc(b_const, 1)
                    one_hot(0, 0)
                    for s in range(S):
                        one_hot((s + 1) // S, (s + 1) % S)
                        add(0, s)
                    with dve.Fori(1, SB - 1) as i:
                        for s in range(S):
                            one_hot(i + (s + 1) // S, (s + 1) % S)
                            add(i, s)
                    for s in range(S):
                        if s + 1 < S:
                            one_hot(SB - 1, s + 1)
                        add(SB - 1, s)

        with ExitStack() as here:
            pass_b(here)

        def outside(dve, chain, cur, rel, base, parts):
            one = cur[:, 1, :]
            chain.link(nc.vector.tensor_scalar(cur[:, 0, :], rel, 0.0, None, ALU.is_lt))
            chain.link(nc.vector.tensor_scalar(one, rel, float(WIN - 1), None, ALU.is_gt))
            chain.link(nc.vector.tensor_tensor(cur[:, 0, :], cur[:, 0, :], one, ALU.add))
            chain.link(nc.vector.tensor_scalar(one, rel, base, 1.0, ALU.add, ALU.add))
            chain.link(nc.vector.tensor_tensor(cur[:, 0, :], cur[:, 0, :], one, ALU.mult))
            chain.link(nc.vector.tensor_scalar(cur[:, 0, :], cur[:, 0, :], -1.0, None, ALU.add))

        with ExitStack() as here:
            h_slot = sb(here, "h_slot", [P, HC])
            m_slot = sb(here, "m_slot", [P, HC])
            msg = sb(here, "msg_g", [P, 6, 2 * D])
            hot = sb(here, "hot_g", [P, 6, WIN])
            cur = sb(here, "cur_g", [P, 2, 6])
            h_in = sem("gb_h_in")
            silu_out = sem("gb_silu_out")
            turned = sem("gb_turned")
            msg_ready = sem("gb_msg_ready")
            hot_ready = sem("gb_hot_ready")
            summed = sem("gb_summed")
            added = sem("gb_added")
            moved_on = sem("gb_moved_on")
            gb_const = sem("gb_const")
            gb_chain = sem("gb_chain")
            with nc.Block() as block:
                @block.sync
                def _(sp):
                    with sp.If(sp.value_load(flag[0:1, 0:1], min_val=0, max_val=1) > 0):
                        with sp.Fori(0, G) as g:
                            sp.wait_ge(silu_out, g + 1)
                            sp.dma_start(h_slot[:, :], h_dram[g]).then_inc(h_in, 16)

                @block.scalar
                def _(act):
                    with act.If(act.value_load(flag[0:1, 0:1], min_val=0, max_val=1) > 0):
                        act.wait_ge(gb_const, 2)
                        act.sem_inc(silu_out, 1)
                        act.sem_inc(msg_ready, 1)
                        with act.Fori(0, G) as g:
                            act.wait_ge(h_in, g * 16 + 16)
                            act.wait_ge(turned, g + 1)
                            act.activation(m_slot[:, :], h_slot[:, :], ACT.Silu, bias=shift1[:, :],
                                           scale=scale1[:, :]).then_inc(silu_out, 1)
                            act.wait_ge(turned, g + 2)
                            act.wait_ge(added, g * NW + 1)
                            act.activation(msg[:, :, D:2 * D],
                                           PS[:, 0, 0:6 * D].rearrange("p (t c) -> p t c", c=D),
                                           ACT.Copy).then_inc(msg_ready, 1)

                @block.tensor
                def _(pe):
                    with pe.If(pe.value_load(flag[0:1, 0:1], min_val=0, max_val=1) > 0):
                        pe.wait_ge(gb_const, 2)
                        pe.sem_inc(turned, 1)
                        pe.sem_inc(summed, 1)
                        with pe.Fori(0, G) as g:
                            pe.wait_ge(silu_out, g + 2)
                            pe.wait_ge(msg_ready, g + 1)
                            for c, (at, n) in enumerate(((0, P), (P, P), (2 * P, D))):
                                last = nc.tensor.transpose(PS[0:n, 0, c * P:(c + 1) * P],
                                                           m_slot[:, at:at + n], ident[:, :])
                            last.then_inc(turned, 1)
                            pe.wait_ge(msg_ready, g + 2)
                            carry_wait(pe)
                            with pe.Fori(0, NW) as w:
                                pe.wait_ge(hot_ready, g * NW + w + 1)
                                pe.wait_ge(added, g * NW + w + 1)
                                for t in range(6):
                                    k = P if t < 4 else D
                                    last = nc.tensor.matmul(PS[:, 1, 0:WIN], msg[0:k, t, :], hot[0:k, t, :],
                                                            start=(t == 0), stop=(t == 5))
                                last.then_inc(summed, 1)

                @block.vector
                def _(dve):
                    with dve.If(dve.value_load(flag[0:1, 0:1], min_val=0, max_val=1) > 0):
                        nc.vector.memset(msg[:, :, 0:D], 1.0).then_inc(gb_const, 1)
                        nc.vector.memset(PS[:, 0, :], 0.0).then_inc(gb_const, 1)
                        dve.sem_inc(added, 1)
                        dve.sem_inc(moved_on, 1)
                        with dve.Fori(0, G) as g:
                            chain = Chain(dve, gb_chain, g * 6)
                            dve.wait_ge(moved_on, g * NW + 1)
                            outside(dve, chain, cur, rel6[:, ds(g, 1), :].rearrange("p a t -> p (a t)"),
                                    base_all[:, ds(g, 1)], P)
                            carry_wait(dve)
                            with dve.Fori(0, NW) as w:
                                dve.wait_ge(summed, g * NW + w + 1)
                                dve.wait_ge(moved_on, g * NW + w + 1)
                                nc.vector.tensor_tensor(
                                    hot[:, :, :], window[:, :].unsqueeze(1).to_broadcast([P, 6, WIN]),
                                    cur[:, 0, :].unsqueeze(2).to_broadcast([P, 6, WIN]),
                                    ALU.is_equal).then_inc(hot_ready, 1)
                                dve.wait_ge(hot_ready, g * NW + w + 1)
                                nc.vector.tensor_scalar(cur[:, 0, :], cur[:, 0, :], -float(WIN), None,
                                                        ALU.add).then_inc(moved_on, 1)
                                dve.wait_ge(summed, g * NW + w + 2)
                                dve.wait_ge(added, g * NW + w + 1)
                                nc.vector.tensor_tensor(table[:, ds(w * WIN, WIN)], table[:, ds(w * WIN, WIN)],
                                                        PS[:, 1, 0:WIN], ALU.add).then_inc(added, 1)

        def layer_norm(chain, z, sq, small, to, root_in, root_out, n):
            mean, varc, rstd = small[:, 0, :], small[:, 1, :], small[:, 2, :]
            wide = [NP, PT, D]
            chain.link(nc.vector.reduce_sum(mean, z, AX))
            chain.link(nc.vector.tensor_scalar(mean, mean, 1.0 / D, None, ALU.mult))
            chain.link(nc.vector.tensor_tensor(z, z, mean.unsqueeze(2).to_broadcast(wide), ALU.subtract))
            chain.link(nc.vector.tensor_tensor(sq, z, z, ALU.mult))
            nc.vector.reduce_sum(varc, sq, AX).then_inc(root_in, 1)
            chain.engine.wait_ge(root_out, n + 1)
            chain.link(nc.vector.reciprocal(rstd, rstd))
            return nc.vector.tensor_tensor(to, z, rstd.unsqueeze(2).to_broadcast(wide), ALU.mult)

        LN_LINKS = 5

        clear_semaphores()

        with ExitStack() as here:
            x_ring = sb(here, "x_ring", [NP, S, CT, D])
            counts = sb(here, "counts", [P, NODES // 4])
            stats = sb(here, "stats_n", [D, CHUNKS * 6])
            moments = sb(here, "moments_n", [D, 2])
            root = sb(here, "root_n", [D, 1])
            act_ring = sb(here, "act_ring", [D, S, CN])
            z = sb(here, "z_n", [NP, PT, D])
            sq = sb(here, "sq_n", [NP, PT, D])
            small = sb(here, "small_n", [NP, 3, PT])
            x1 = sb(here, "x1_n", [NP, PT, D])
            eps1c = sb(here, "eps1c", [D, 1])

            x_loaded = sems("x_loaded")
            x_turned = sems("x_turned")
            counts_done = sem("counts_done")
            count_chain = sem("count_chain")
            xT_ready = sem("xT_ready")
            h2_put = sem("h2_put")
            h2_ready = sem("h2_ready")
            h2_stats = sem("h2_stats")
            n_chain = sem("n_chain")
            var2_in = sem("var2_in")
            root2 = sem("root2")
            bn2_ready = sem("bn2_ready")
            act_ready = sems("act_ready")
            act_turned = sems("act_turned")
            z_ready = sem("z_ready")
            ln_chain = sem("ln_chain")
            ln_in = sem("ln_in")
            ln_root = sem("ln_root")
            x1_ready = sem("x1_ready")
            x1_kept = sem("x1_kept")
            x1_stored = sem("x1_stored")
            x1_turned = sem("x1_turned")
            x1T_ready = sem("x1T_ready")
            eps_chain = sem("eps_chain")

            with nc.Block() as block:
                @block.sync
                def _(sp):
                    def turn(i):
                        for s in range(S):
                            reuse(sp, x_turned[s], i)
                            sp.dma_start(x_ring[:, s, :, :], x_v[:, ds((i * S + s) * CT, CT), :]
                                         ).then_inc(x_loaded[s], 16)

                    turn(0)
                    with sp.Fori(1, PIECES) as i:
                        turn(i)
                    def turn(i):
                        sp.wait_ge(x1_ready, i + 1)
                        sp.dma_start(x1_v[:, ds(i * (PT * D), PT * D)],
                                     x1[:, :, :].rearrange("p t c -> p (t c)")).then_inc(x1_stored, 16)

                    turn(0)
                    with sp.Fori(1, PIECES) as i:
                        turn(i)
                    sp.wait_ge(x1_stored, 16 * PIECES)

                @block.tensor
                def _(pe):
                    def turn(i):
                        for s in range(S):
                            k = i * S + s
                            pe.wait_ge(x_loaded[s], i * 16 + 16)
                            reuse(pe, xT_ready, i * S + max(s - 1, 0))
                            carry_wait(pe)
                            for t in range(CT):
                                last = nc.tensor.transpose(PS[0:D, s % 2, t * NP:(t + 1) * NP],
                                                           x_ring[:, s, t, :], ident[0:NP, 0:NP])
                            last.then_inc(x_turned[s], 1)
                            pe.wait_ge(xT_ready, k + 1)
                            reuse(pe, h2_ready, i * S + max(s - 1, 0))
                            nc.tensor.matmul(PS[0:D, 2 + s % 2, 0:CN].rearrange("f (t p) -> f t p", t=CT),
                                             W2_sb[:, :], table_t[:, ds(k * CT, CT), :],
                                             start=True, stop=True).then_inc(h2_put, 1)

                    turn(0)
                    with pe.Fori(1, PIECES) as i:
                        turn(i)
                    def turn(i):
                        reuse(pe, z_ready, i)
                        for s in range(S):
                            pe.wait_ge(act_ready[s], i + 1)
                            carry_wait(pe)
                            for t in range(CT):
                                n = s * CT + t
                                last = nc.tensor.transpose(banks(0, 3, NP, PT * D)[:, n * D:(n + 1) * D],
                                                           act_ring[:, s, t * NP:(t + 1) * NP], ident[0:D, 0:D])
                            last.then_inc(act_turned[s], 1)
                        pe.wait_ge(x1_ready, i + 1)
                        reuse(pe, x1T_ready, i * S)
                        carry_wait(pe)
                        for s in range(S):
                            for t in range(CT):
                                last = nc.tensor.transpose(PS[0:D, 3 + s, t * NP:(t + 1) * NP],
                                                           x1[:, s * CT + t, :], ident[0:NP, 0:NP])
                        last.then_inc(x1_turned, 1)

                    turn(0)
                    with pe.Fori(1, PIECES) as i:
                        turn(i)

                @block.scalar
                def _(act):
                    act.wait_ge(counts_done, 1)
                    def turn(i):
                        for s in range(S):
                            k = i * S + s
                            here_t = table_t[0:D, ds(k * CT, CT), :]
                            act.wait_ge(x_turned[s], i + 1)
                            carry_wait(act)
                            act.activation(here_t, PS[0:D, s % 2, 0:CN].rearrange("f (t p) -> f t p", t=CT),
                                           ACT.Copy).then_inc(xT_ready, 1)
                            act.wait_ge(h2_put, k + 1)
                            carry_wait(act)
                            act.activation(here_t, PS[0:D, 2 + s % 2, 0:CN].rearrange("f (t p) -> f t p", t=CT),
                                           ACT.Identity, bias=b2c[:, :]).then_inc(h2_ready, 1)

                    turn(0)
                    with act.Fori(1, PIECES) as i:
                        turn(i)
                    act.wait_ge(var2_in, 1)
                    act.activation(root[:, :], moments[:, 1:2], ACT.Sqrt, bias=epsP[0:D, :]).then_inc(root2, 1)
                    act.wait_ge(bn2_ready, 1)
                    def turn(i):
                        for s in range(S):
                            reuse(act, act_turned[s], i)
                            carry_wait(act)
                            act.activation(act_ring[:, s, :].rearrange("f (t p) -> f t p", t=CT),
                                           table_t[0:D, ds((i * S + s) * CT, CT), :], ACT.Silu,
                                           bias=shift2[:, :], scale=scale2[:, :]).then_inc(act_ready[s], 1)
                        act.wait_ge(ln_in, i + 1)
                        act.activation(small[:, 2, :], small[:, 1, :], ACT.Sqrt, bias=epsP[0:NP, :],
                                       scale=1.0 / D).then_inc(ln_root, 1)
                        act.wait_ge(x1_ready, i + 1)
                        carry_wait(act)
                        act.activation(x3[:, ds(i * PT, PT), :], x1[:, :, :], ACT.Copy).then_inc(x1_kept, 1)
                        act.wait_ge(x1_turned, i + 1)
                        carry_wait(act)
                        for s in range(S):
                            act.activation(table_t[0:D, ds((i * S + s) * CT, CT), :],
                                           PS[0:D, 3 + s, 0:CN].rearrange("f (t p) -> f t p", t=CT),
                                           ACT.Identity, scale=eps1c[:, :]).then_inc(x1T_ready, 1)

                    turn(0)
                    with act.Fori(1, PIECES) as i:
                        turn(i)

                @block.vector
                def _(dve):
                    chain = Chain(dve, count_chain)
                    quarter = NODES // 4
                    for n in range(4):
                        c, m = table[0:D, n * quarter:(n + 1) * quarter], table[D:P, n * quarter:(n + 1) * quarter]
                        chain.link(nc.vector.tensor_scalar(c, c, 1.0, None, ALU.max))
                        chain.link(nc.vector.reciprocal(counts[D:P, :], c))
                        chain.link(nc.vector.tensor_tensor(m, m, counts[D:P, :], ALU.mult))
                    nc.vector.tensor_scalar(eps1c[:, :], eps_c[:, :], 1.0, None, ALU.add).then_inc(counts_done, 1)
                    def turn(i):
                        for s in range(S):
                            k = i * S + s
                            dve.wait_ge(h2_ready, k + 1)
                            nc.vector.bn_stats(stats[:, ds(k * 6, 6)], table_t[0:D, ds(k * CT, CT), :]
                                               ).then_inc(h2_stats, 1)

                    turn(0)
                    with dve.Fori(1, PIECES) as i:
                        turn(i)
                    dve.wait_ge(h2_stats, CHUNKS)
                    nc.vector.bn_aggr(moments[:, :], stats[:, :]).then_inc(var2_in, 1)
                    dve.wait_ge(root2, 1)
                    chain = Chain(dve, n_chain)
                    chain.link(nc.vector.reciprocal(root[:, :], root[:, :]))
                    chain.link(nc.vector.tensor_tensor(scale2[:, :], root[:, :], g2c[:, :], ALU.mult))
                    chain.link(nc.vector.tensor_tensor(root[:, :], moments[:, 0:1], scale2[:, :], ALU.mult))
                    nc.vector.tensor_tensor(shift2[:, :], be2c[:, :], root[:, :], ALU.subtract).then_inc(bn2_ready, 1)
                    def turn(i):
                        dve.wait_ge(act_turned[S - 1], i + 1)
                        reuse(dve, x1_ready, i)
                        nc.vector.tensor_tensor(z[:, :, :], x3[:, ds(i * PT, PT), :],
                                                banks(0, 3, NP, PT * D).rearrange("p (t c) -> p t c", c=D),
                                                ALU.add).then_inc(z_ready, 1)
                        dve.wait_ge(z_ready, i + 1)
                        reuse(dve, x1_kept, i)
                        reuse(dve, x1_turned, i)
                        reuse(dve, x1_stored, i * 16)
                        layer_norm(Chain(dve, ln_chain, i * LN_LINKS), z[:, :, :], sq[:, :, :], small,
                                   x1[:, :, :], ln_in, ln_root, i).then_inc(x1_ready, 1)

                    turn(0)
                    with dve.Fori(1, PIECES) as i:
                        turn(i)

        clear_semaphores()

        with ExitStack() as here:
            E = sb(here, "E", [P, S, TG, D])
            X = sb(here, "X", [P, S, TG, D])
            msg = sb(here, "msg_c", [P, S, TG, D])
            hot = sb(here, "hot_c", [P, S, TG, WIN])
            e_loaded = sems("c_e_loaded")
            gathered = gathered_x1
            sum_ready = sems("sum_ready")
            idx_ready = sems("c_idx_ready")
            hot_ready = sems("c_hot_ready")
            msg_ready = sems("c_msg_ready")
            summed = sems("c_summed")
            added = sem("c_added")
            idx_first = sem("idx_first")

            with nc.Block() as block:
                @block.sync
                def _(sp):
                    def turn(i):
                        for s in range(S):
                            reuse(sp, msg_ready[s], i)
                            sp.dma_start(E[:, s, :, :], edge_v[i * S + s]).then_inc(e_loaded[s], 16)

                    turn(0)
                    with sp.Fori(1, SB) as i:
                        turn(i)

                @block.gpsimd
                def _(pool):
                    pool.wait_ge(idx_first, 1)
                    def turn(i):
                        for s in range(S):
                            reuse(pool, idx_ready[s], i)
                            reuse(pool, sum_ready[s], i)
                            carry_wait(pool)
                            for j in range(TG):
                                nc.gpsimd.indirect_dma_start(
                                    out=X[:, s, j, :], out_offset=None, in_=x1_dram,
                                    in_offset=bass.IndirectOffsetOnAxis(ap=idx_ring[:, s, j:j + 1], axis=0)
                                ).then_inc(gathered[s], 16)

                    turn(0)
                    with pool.Fori(1, SB) as i:
                        turn(i)

                @block.scalar
                def _(act):
                    def turn(i):
                        for s in range(S):
                            act.wait_ge(sum_ready[s], i + 1)
                            reuse(act, summed[s], i)
                            act.activation(msg[:, s, :, :], E[:, s, :, :], ACT.Relu).then_inc(msg_ready[s], 1)

                    turn(0)
                    with act.Fori(1, SB) as i:
                        turn(i)

                @block.tensor
                def _(pe):
                    def turn(i):
                        for s in range(S):
                            pe.wait_ge(msg_ready[s], i + 1)
                            pe.wait_ge(hot_ready[s], i + 1)
                            reuse(pe, added, i * S + max(s - 1, 0))
                            for j in range(TG):
                                last = nc.tensor.matmul(PS[0:D, s % 2, 0:WIN], msg[:, s, j, :], hot[:, s, j, :],
                                                        start=(j == 0), stop=(j == TG - 1))
                            last.then_inc(summed[s], 1)

                    turn(0)
                    with pe.Fori(1, SB) as i:
                        turn(i)

                @block.vector
                def _(dve):
                    nc.vector.tensor_copy(idx_flat, src_idx[:, 0:S * TG]).then_inc(idx_first, 1)
                    def turn(i):
                        for s in range(S):
                            g = i * S + s
                            first = dve.value_load(base_row[0:1, ds(g, 1)], min_val=0, max_val=NODES - 1)
                            reuse(dve, summed[s], i)
                            nc.vector.tensor_tensor(
                                hot[:, s, :, :], window[:, :].unsqueeze(1).to_broadcast([P, TG, WIN]),
                                rel5[:, ds(g, 1), :].rearrange("p a t -> p (a t)").unsqueeze(2)
                                .to_broadcast([P, TG, WIN]), ALU.is_equal).then_inc(hot_ready[s], 1)
                            dve.wait_ge(e_loaded[s], i * 16 + 16)
                            dve.wait_ge(gathered[s], i * (16 * TG) + 16 * TG)
                            nc.vector.tensor_tensor(E[:, s, :, :], X[:, s, :, :], E[:, s, :, :],
                                                    ALU.add).then_inc(sum_ready[s], 1)
                            nc.vector.tensor_copy(idx_ring[:, s, :],
                                                  src_idx[:, ds(i * (S * TG) + (S + s) * TG, TG)]
                                                  ).then_inc(idx_ready[s], 1)
                            dve.wait_ge(summed[s], i + 1)
                            reuse(dve, added, g)
                            nc.vector.tensor_tensor(table[0:D, ds(first, WIN)], table[0:D, ds(first, WIN)],
                                                    PS[0:D, s % 2, 0:WIN], ALU.add).then_inc(added, 1)

                    turn(0)
                    with dve.Fori(1, SB) as i:
                        turn(i)

        with ExitStack() as here:
            E = sb(here, "E_g", [P, TG, D])
            X = sb(here, "X_g", [P, TG, D])
            msg = sb(here, "msg_h", [P, TG, D])
            hot = sb(here, "hot_h", [P, TG, WIN])
            cur = sb(here, "cur_h", [P, 2, TG])
            e_in = sem("gc_e_in")
            idx_in = sem("gc_idx_in")
            rows_in = gathered_general
            sum_in = sem("gc_sum_in")
            msg_ready = sem("gc_msg_ready")
            hot_ready = sem("gc_hot_ready")
            summed = sem("gc_summed")
            added = sem("gc_added")
            moved_on = sem("gc_moved_on")
            gc_chain = sem("gc_chain")
            with nc.Block() as block:
                @block.sync
                def _(sp):
                    with sp.If(sp.value_load(flag[0:1, 0:1], min_val=0, max_val=1) > 0):
                        with sp.Fori(0, G) as g:
                            sp.wait_ge(msg_ready, g + 1)
                            sp.dma_start(E[:, :, :], edge_v[g]).then_inc(e_in, 16)

                @block.gpsimd
                def _(pool):
                    with pool.If(pool.value_load(flag[0:1, 0:1], min_val=0, max_val=1) > 0):
                        with pool.Fori(0, G) as g:
                            pool.wait_ge(idx_in, g + 1)
                            carry_wait(pool)
                            for j in range(TG):
                                nc.gpsimd.indirect_dma_start(
                                    out=X[:, j, :], out_offset=None, in_=x1_dram,
                                    in_offset=bass.IndirectOffsetOnAxis(ap=idx_ring[:, 0, j:j + 1], axis=0)
                                ).then_inc(rows_in, 16)

                @block.scalar
                def _(act):
                    with act.If(act.value_load(flag[0:1, 0:1], min_val=0, max_val=1) > 0):
                        act.sem_inc(msg_ready, 1)
                        with act.Fori(0, G) as g:
                            act.wait_ge(sum_in, g + 1)
                            act.wait_ge(added, g * NW + 1)
                            act.activation(msg[:, :, :], E[:, :, :], ACT.Relu).then_inc(msg_ready, 1)

                @block.tensor
                def _(pe):
                    with pe.If(pe.value_load(flag[0:1, 0:1], min_val=0, max_val=1) > 0):
                        pe.sem_inc(summed, 1)
                        with pe.Fori(0, G) as g:
                            pe.wait_ge(msg_ready, g + 2)
                            carry_wait(pe)
                            with pe.Fori(0, NW) as w:
                                pe.wait_ge(hot_ready, g * NW + w + 1)
                                pe.wait_ge(added, g * NW + w + 1)
                                for j in range(TG):
                                    last = nc.tensor.matmul(PS[0:D, 1, 0:WIN], msg[:, j, :], hot[:, j, :],
                                                            start=(j == 0), stop=(j == TG - 1))
                                last.then_inc(summed, 1)

                @block.vector
                def _(dve):
                    with dve.If(dve.value_load(flag[0:1, 0:1], min_val=0, max_val=1) > 0):
                        dve.sem_inc(added, 1)
                        dve.sem_inc(moved_on, 1)
                        with dve.Fori(0, G) as g:
                            nc.vector.tensor_copy(idx_ring[:, 0, :], src_idx[:, ds(g * TG, TG)]).then_inc(idx_in, 1)
                            dve.wait_ge(e_in, g * 16 + 16)
                            dve.wait_ge(rows_in, g * (16 * TG) + 16 * TG)
                            nc.vector.tensor_tensor(E[:, :, :], X[:, :, :], E[:, :, :], ALU.add).then_inc(sum_in, 1)
                            chain = Chain(dve, gc_chain, g * 6)
                            dve.wait_ge(moved_on, g * NW + 1)
                            outside(dve, chain, cur, rel5[:, ds(g, 1), :].rearrange("p a t -> p (a t)"),
                                    base_all[:, ds(g, 1)], P)
                            carry_wait(dve)
                            with dve.Fori(0, NW) as w:
                                dve.wait_ge(summed, g * NW + w + 1)
                                dve.wait_ge(moved_on, g * NW + w + 1)
                                nc.vector.tensor_tensor(
                                    hot[:, :, :], window[:, :].unsqueeze(1).to_broadcast([P, TG, WIN]),
                                    cur[:, 0, :].unsqueeze(2).to_broadcast([P, TG, WIN]),
                                    ALU.is_equal).then_inc(hot_ready, 1)
                                dve.wait_ge(hot_ready, g * NW + w + 1)
                                nc.vector.tensor_scalar(cur[:, 0, :], cur[:, 0, :], -float(WIN), None,
                                                        ALU.add).then_inc(moved_on, 1)
                                dve.wait_ge(summed, g * NW + w + 2)
                                dve.wait_ge(added, g * NW + w + 1)
                                nc.vector.tensor_tensor(table[0:D, ds(w * WIN, WIN)], table[0:D, ds(w * WIN, WIN)],
                                                        PS[0:D, 1, 0:WIN], ALU.add).then_inc(added, 1)

        clear_semaphores()

        with ExitStack() as here:
            act_ring = sb(here, "act_ring_o", [D, S, CN])
            z = sb(here, "z_o", [NP, PT, D])
            sq = sb(here, "sq_o", [NP, PT, D])
            small = sb(here, "small_o", [NP, 3, PT])
            y = sb(here, "y", [NP, PT, D])
            lin_put = sems("lin_put")
            act_ready = sems("o_act_ready")
            act_turned = sems("o_act_turned")
            z_ready = sem("o_z_ready")
            ln_chain = sem("o_ln_chain")
            ln_in = sem("o_ln_in")
            ln_root = sem("o_ln_root")
            y_ready = sem("y_ready")
            y_stored = sem("y_stored")
            with nc.Block() as block:
                @block.sync
                def _(sp):
                    def turn(i):
                        sp.wait_ge(y_ready, i + 1)
                        sp.dma_start(out_v[:, ds(i * (PT * D), PT * D)],
                                     y[:, :, :].rearrange("p t c -> p (t c)")).then_inc(y_stored, 16)

                    turn(0)
                    with sp.Fori(1, PIECES) as i:
                        turn(i)
                    sp.wait_ge(y_stored, 16 * PIECES)

                @block.tensor
                def _(pe):
                    def turn(i):
                        for s in range(S):
                            reuse(pe, act_ready[s], i)
                            nc.tensor.matmul(PS[:, 3 + s, 0:CN].rearrange("f (t p) -> f t p", t=CT), W3T[:, :],
                                             table_t[0:D, ds((i * S + s) * CT, CT), :],
                                             start=True, stop=True).then_inc(lin_put[s], 1)
                        reuse(pe, z_ready, i)
                        for s in range(S):
                            pe.wait_ge(act_ready[s], i + 1)
                            carry_wait(pe)
                            for t in range(CT):
                                n = s * CT + t
                                last = nc.tensor.transpose(banks(0, 3, NP, PT * D)[:, n * D:(n + 1) * D],
                                                           act_ring[:, s, t * NP:(t + 1) * NP], ident[0:D, 0:D])
                            last.then_inc(act_turned[s], 1)

                    turn(0)
                    with pe.Fori(1, PIECES) as i:
                        turn(i)

                @block.scalar
                def _(act):
                    def turn(i):
                        for s in range(S):
                            act.wait_ge(lin_put[s], i + 1)
                            reuse(act, act_turned[s], i)
                            act.activation(act_ring[:, s, :], PS[0:D, 3 + s, 0:CN], ACT.Relu,
                                           bias=b3c[:, :]).then_inc(act_ready[s], 1)
                        act.wait_ge(ln_in, i + 1)
                        act.activation(small[:, 2, :], small[:, 1, :], ACT.Sqrt, bias=epsP[0:NP, :],
                                       scale=1.0 / D).then_inc(ln_root, 1)

                    turn(0)
                    with act.Fori(1, PIECES) as i:
                        turn(i)

                @block.vector
                def _(dve):
                    def turn(i):
                        dve.wait_ge(act_turned[S - 1], i + 1)
                        reuse(dve, y_ready, i)
                        nc.vector.tensor_tensor(z[:, :, :], x3[:, ds(i * PT, PT), :],
                                                banks(0, 3, NP, PT * D).rearrange("p (t c) -> p t c", c=D),
                                                ALU.add).then_inc(z_ready, 1)
                        dve.wait_ge(z_ready, i + 1)
                        reuse(dve, y_stored, i * 16)
                        layer_norm(Chain(dve, ln_chain, i * LN_LINKS), z[:, :, :], sq[:, :, :], small,
                                   y[:, :, :], ln_in, ln_root, i).then_inc(y_ready, 1)

                    turn(0)
                    with dve.Fori(1, PIECES) as i:
                        turn(i)


_INS = ['x', 'src', 'dst', 'edge_attr_64', 'L0_gnn_W1', 'L0_gnn_b1', 'L0_gnn_g1', 'L0_gnn_be1',
        'L0_gnn_W2', 'L0_gnn_b2', 'L0_gnn_g2', 'L0_gnn_be2', 'L1_gnn_W', 'L1_gnn_b', 'L1_gnn_eps']


def kernel(**inputs):
    import numpy as _np
    import concourse.bacc as _bacc
    from concourse import mybir as _mybir
    from concourse.bass_utils import run_bass_kernel_spmd as _run

    nc = _bacc.Bacc("TRN2", target_bir_lowering=False, num_devices=1)
    arrays, args = {}, []
    for name in _INS:
        a = _np.ascontiguousarray(inputs[name])
        if a.ndim == 0:
            a = a.reshape(1)
        arrays[f"in_{name}_dram"] = a
        args.append(nc.dram_tensor(f"in_{name}_dram", a.shape, _mybir.dt.from_np(a.dtype), kind="ExternalInput").ap())
    args.append(nc.dram_tensor("out_dram", inputs["x"].shape, _mybir.dt.float32, kind="ExternalOutput").ap())
    gnn_kernel(nc, *args)
    r = _run(nc, [arrays], core_ids=[0])
    return r.results[0]["out_dram"]
```

```python
import concourse.bass as bass
from concourse import mybir
from contextlib import ExitStack



class Chain:

    def __init__(self, engine, sem, base=0):
        self.engine, self.sem, self.base, self.n = engine, sem, base, 0

    def link(self, instruction):
        self.n += 1
        instruction.then_inc(self.sem, 1)
        self.engine.wait_ge(self.sem, self.base + self.n)


def reuse(engine, sem, n):
    if not (isinstance(n, int) and n == 0):
        engine.wait_ge(sem, n)


def loop_halves(engine, first, end, turn):
    rounds = (end - first) // 2
    with engine.Fori(0, rounds) as k:
        for u in (0, 1):
            turn(k * 2 + (first + u), (first + u) % 2, k + (first + u) // 2)
    for i in range(first + 2 * rounds, end):
        turn(i, i % 2, i // 2)


def gnn_kernel(nc, x, src, dst, edge, W1, b1, g1, be1, W2, b2, g2, be2, W3, b3, eps1, out):
    fp32 = mybir.dt.float32
    int32 = mybir.dt.int32
    bf16 = mybir.dt.bfloat16
    ALU = mybir.AluOpType
    ACT = mybir.ActivationFunctionType
    AX = mybir.AxisListType.X
    ds = bass.ds

    P = 128
    NODES, D = x.shape
    EDGES = edge.shape[0]
    EPS = 1e-5
    TG = 5
    EG = TG * P
    S = 5
    G = EDGES // EG
    SB = G // S
    WIN = 48
    NW = -(-NODES // WIN)
    HC = TG * D
    NP = 125
    NT = NODES // NP
    CT = 4
    CN = CT * NP
    PT = S * CT
    PIECES = NT // PT
    CHUNKS = NT // CT
    TABLE_POOL = 3 * NODES // 4
    assert EDGES == G * EG and G == SB * S and SB <= P and NODES == NP * NT and NT == PIECES * PT

    edge_v = edge.rearrange("(g p j) c -> g p j c", p=P, j=TG)
    src_v = src.rearrange("(sb n) -> sb n", sb=SB)
    dst_v = dst.rearrange("(sb n) -> sb n", sb=SB)
    first_v = dst.rearrange("(o g n) -> o g n", o=1, n=EG)[:, :, 0]
    x_v = x.rearrange("(p t) c -> p t c", p=NP)
    out_v = out.rearrange("(p t) c -> p (t c)", p=NP)
    h_dram = nc.dram_tensor("h_scratch", (G, P, HC), fp32, kind="Internal").ap()
    x1_dram = nc.dram_tensor("x1_scratch", (NODES, D), fp32, kind="Internal").ap()
    counts_dram = nc.dram_tensor("counts_scratch", (NODES,), fp32, kind="Internal").ap()
    shares_dram = nc.dram_tensor("shares_scratch", (NODES,), fp32, kind="Internal").ap()
    x1_v = x1_dram.rearrange("(p t) c -> p (t c)", p=NP)

    def col(v):
        return v.rearrange("(a b) -> a b", b=1)

    ctx = ExitStack()
    with ctx:
        def sb(where, name, shape, dt=fp32):
            return where.enter_context(nc.sbuf_tensor(name, shape, dt))

        in_use = []

        def sem(name):
            in_use.append(nc.alloc_semaphore(name))
            return in_use[-1]

        def sems(name):
            return [sem(f"{name}{s}") for s in range(S)]

        def clear_semaphores():
            nc.clear_and_free_semaphores(list(in_use))
            nc.all_engine_barrier()
            in_use.clear()

        steps = ctx.enter_context(nc.semaphore("steps"))

        def carry_wait(engine):
            engine.sem_inc(steps, 1)

        gathered_x = [ctx.enter_context(nc.semaphore(f"gathered_x{s}")) for s in range(S)]
        gathered_x1 = [ctx.enter_context(nc.semaphore(f"gathered_x1{s}")) for s in range(S)]
        gathered_general = ctx.enter_context(nc.semaphore("gathered_general"))

        table = sb(ctx, "table", [P, NODES + WIN])
        x_nodes = sb(ctx, "x_nodes", [NP, NT * D])
        src_idx = sb(ctx, "src_idx", [P, (SB + 1) * S * TG], int32)
        rel5 = sb(ctx, "rel5", [P, G, TG])
        base_all = sb(ctx, "base_all", [P, G])
        base_row = sb(ctx, "base_row", [1, SB, 8], int32)
        idx_ring = sb(ctx, "idx_ring", [P, S, TG], int32)
        ident = sb(ctx, "ident", [P, P])
        halves = sb(ctx, "halves", [P, P])
        window = sb(ctx, "window", [P, WIN])
        flag = sb(ctx, "flag", [1, 1], int32)
        W1_sb = sb(ctx, "W1_sb", [2 * D, D])
        W2_sb = sb(ctx, "W2_sb", [2 * D, D])
        W3T = sb(ctx, "W3T", [2 * D, D])
        b1c = sb(ctx, "b1c", [P, 1])
        g1c = sb(ctx, "g1c", [P, 1])
        be1c = sb(ctx, "be1c", [P, 1])
        b2c = sb(ctx, "b2c", [D, 1])
        g2c = sb(ctx, "g2c", [D, 1])
        be2c = sb(ctx, "be2c", [D, 1])
        b3c = sb(ctx, "b3c", [D, 1])
        eps_c = sb(ctx, "eps_c", [P, 1])
        scale1 = sb(ctx, "scale1", [P, D])
        shift1 = sb(ctx, "shift1", [P, D])
        b1_row = sb(ctx, "b1_row", [P, D])
        scale2 = sb(ctx, "scale2", [D, 1])
        shift2 = sb(ctx, "shift2", [D, 1])
        epsP = sb(ctx, "epsP", [P, 1])
        PS = ctx.enter_context(nc.psum_tensor("PS", [P, 8, 512], fp32))

        def banks(first, n, parts, cols):
            return PS[0:parts, first:first + n, :].rearrange("p b c -> p (b c)")[:, 0:cols]

        x3 = x_nodes[:, :].rearrange("p (t c) -> p t c", c=D)
        table_t = table[:, 0:NODES].rearrange("f (p t) -> f t p", t=NT)
        idx_flat = idx_ring[:, :, :].rearrange("p s j -> p (s j)")

        window_regs = [nc.vector.alloc_register(f"window_reg{s}") for s in range(S)]

        def load_windows(dve, i):
            dve.load(window_regs, base_row[0:1, ds(i, 1), 0:S].rearrange("o a q -> o (a q)"))

        def windows_of_turn(dve):
            return [dve.snap(reg, min_val=0, max_val=NODES - 1) for reg in window_regs]

        def index_tiles(rows):
            return rows[:, :].bitcast(fp32).rearrange("sb (q p j) -> sb q j p", q=S, j=TG)

        def turn_indices(pe, n, q, tiles, put):
            for j in range(TG):
                to = banks(2 * (n % 2), 2, P, TG * P)[:, j * P:j * P + SB]
                last = nc.tensor.transpose(to, tiles[:, q, j, :], ident[0:SB, 0:SB])
            last.then_inc(put, 1)

        def take_indices(n, q, to):
            put = banks(2 * (n % 2), 2, P, TG * P).rearrange("p (j c) -> p j c", j=TG)
            return nc.vector.tensor_copy(to.rearrange("p (sb q j) -> p q j sb", q=S, j=TG)[:, q, :, :],
                                         put[:, :, 0:SB])

        s_x = sem("s_x")
        s_w = sem("s_w")
        s_dst = sem("s_dst")
        s_first = sem("s_first")
        WEIGHTS = 16

        with ExitStack() as here:
            dst_rows = sb(here, "dst_rows", [SB, S * EG], int32)
            base_in = sb(here, "base_in", [1, G], int32)
            base_f = sb(here, "base_f", [1, G])
            ones_row = sb(here, "ones_row", [1, P])
            ones_col = sb(here, "ones_col", [P, 1])
            W3_sb = sb(here, "W3_sb", [D, 2, D])

            with ExitStack() as prep:
                src_rows = sb(prep, "src_rows", [SB, S * EG], int32)
                iota_i = sb(prep, "iota_i", [P, WIN], int32)
                s_src = sem("s_src")
                s_zero = sem("s_zero")
                s_ident = sem("s_ident")
                s_iota = sem("s_iota")
                s_const = sem("s_const")
                src_float = sem("src_float")
                pieces_put = sem("pieces_put")
                pieces_taken = sem("pieces_taken")

                with nc.Block() as block:
                    @block.sync
                    def _(sp):
                        sp.dma_start(src_rows[:, :], src_v).then_inc(s_src, 16)
                        sp.dma_start(dst_rows[:, :], dst_v).then_inc(s_dst, 16)
                        sp.dma_start(base_in[:, :], first_v, allow_slow_non_contiguous=True).then_inc(s_first, 16)
                        sp.dma_start(x_nodes[:, :], x_v.rearrange("p t c -> p (t c)")).then_inc(s_x, 16)

                    @block.scalar
                    def _(act):
                        for to, of in ((W3_sb[:, 0, :], W3), (W3_sb[:, 1, :], W3), (W1_sb[:, :], W1), (b1_row[:, :], b1.partition_broadcast(P)),
                                       (b1c[0:D, :], col(b1)), (b1c[D:P, :], col(b1)),
                                       (g1c[0:D, :], col(g1)), (g1c[D:P, :], col(g1)),
                                       (be1c[0:D, :], col(be1)), (be1c[D:P, :], col(be1)),
                                       (W2_sb[:, :], W2), (b2c[:, :], col(b2)), (g2c[:, :], col(g2)),
                                       (be2c[:, :], col(be2)), (b3c[:, :], col(b3)),
                                       (eps_c[:, :], eps1.partition_broadcast(P))):
                            act.dma_start(to, of).then_inc(s_w, 16)

                    @block.gpsimd
                    def _(pool):
                        nc.gpsimd.memset(ident[:, :], 0.0).then_inc(s_zero, 1)
                        pool.wait_ge(s_zero, 1)
                        nc.gpsimd.affine_select(out=ident[:, :], in_=ident[:, :], compare_op=ALU.not_equal,
                                                fill=1.0, base=0, pattern=[[-1, P]],
                                                channel_multiplier=1).then_inc(s_ident, 1)
                        nc.gpsimd.memset(ones_row[:, :], 1.0)
                        nc.gpsimd.memset(ones_col[:, :], 1.0)
                        nc.gpsimd.memset(epsP[:, :], EPS)
                        nc.gpsimd.memset(src_idx[:, G * TG:], 0)
                        nc.gpsimd.iota(iota_i[:, :], pattern=[[1, WIN]], base=0,
                                       channel_multiplier=0).then_inc(s_iota, 1)
                        pool.wait_ge(s_iota, 1)
                        nc.gpsimd.tensor_copy(window[:, :], iota_i[:, :]).then_inc(s_const, 1)
                        nc.gpsimd.memset(table[:, 0:TABLE_POOL], 0.0)

                    @block.tensor
                    def _(pe):
                        pe.wait_ge(s_ident, 1)
                        for q in range(S):
                            pe.wait_ge(src_float, q + 1)
                            if q >= 2:
                                pe.wait_ge(pieces_taken, q - 1)
                            turn_indices(pe, q, q, index_tiles(src_rows), pieces_put)

                    @block.vector
                    def _(dve):
                        nc.vector.memset(table[:, TABLE_POOL:], 0.0)
                        dve.wait_ge(s_src, 16)
                        for q in range(S):
                            part = src_rows[:, q * EG:(q + 1) * EG]
                            nc.vector.tensor_copy(part.bitcast(fp32), part).then_inc(src_float, 1)
                        dve.wait_ge(s_const, 1)
                        for q in range(S):
                            dve.wait_ge(pieces_put, q + 1)
                            take_indices(q, q, src_idx[:, 0:G * TG]).then_inc(pieces_taken, 1)
                        dve.wait_ge(pieces_taken, S)
                        nc.vector.tensor_copy(idx_flat, src_idx[:, 0:S * TG])

            most = sb(here, "most", [P, 1])
            least = sb(here, "least", [P, 1])
            bad = sb(here, "bad", [P, 1])
            flag_f = sb(here, "flag_f", [1, 1])
            Z = sb(here, "Z", [P, S, TG, 2 * D])
            ZT = sb(here, "ZT", [P, EG])
            h_ring = sb(here, "h_ring", [P, S, TG, D])
            spread = sb(here, "spread", [D, 2, D])
            scale_col = sb(here, "scale_col", [P, 1])
            shift_col = sb(here, "shift_col", [P, 1])
            ones_f = sb(here, "ones_f", [D, P])
            stats = sb(here, "stats", [P, G * 6])
            moments = sb(here, "moments", [P, 2])
            mean = sb(here, "mean", [P, 1])
            off = sb(here, "off", [P, 1])
            var = sb(here, "var", [P, 1])
            ones_bf = sb(here, "ones_bf", [P, D], bf16)
            hot = sb(here, "hot_a", [P, S, TG, WIN], bf16)

            dst_float = sem("dst_float")
            first_float = sem("first_float")
            dst_put = sem("dst_put")
            dst_taken = sem("dst_taken")
            base_put = sem("base_put")
            w3_put = sem("w3_put")
            bad_ready = sem("bad_ready")
            bad_sum = sem("bad_sum")
            windows_ready = sem("windows_ready")
            prep_chain = sem("prep_chain")
            hot_ready = sems("a_hot_ready")
            count_added = sem("count_added")
            e_loaded = sems("e_loaded")
            gathered = gathered_x
            rows_done = sems("rows_done")
            zt_taken = sem("zt_taken")
            ht_put = sem("ht_put")
            h_put = sem("h_put")
            h_ready = sems("h_ready")
            h_stored = sems("h_stored")
            stats_done = sem("stats_done")
            spread_ready = sem("spread_ready")
            rows_put = sem("rows_put")
            idx_ready = sems("idx_ready")
            mean_in = sem("mean_in")
            mean_put = sem("mean_put")
            var_in = sem("var_in")
            var_put = sem("var_put")
            var_sb = sem("var_sb")
            root1 = sem("root1")
            a_chain = sem("a_chain")

            with nc.Block() as block:
                @block.sync
                def _(sp):
                    def turn(i):
                        for s in range(S):
                            reuse(sp, rows_done[s], i)
                            sp.dma_start(Z[:, s, :, D:2 * D], edge_v[i * S + s]).then_inc(e_loaded[s], 16)

                    turn(0)
                    with sp.Fori(1, SB) as i:
                        turn(i)
                    sp.wait_ge(s_x, 16)

                @block.gpsimd
                def _(pool):
                    def turn(i):
                        for s in range(S):
                            reuse(pool, idx_ready[s], i)
                            reuse(pool, rows_done[s], i)
                            carry_wait(pool)
                            for j in range(TG):
                                nc.gpsimd.indirect_dma_start(
                                    out=Z[:, s, j, 0:D], out_offset=None, in_=x,
                                    in_offset=bass.IndirectOffsetOnAxis(ap=idx_ring[:, s, j:j + 1], axis=0)
                                ).then_inc(gathered[s], 16)

                    turn(0)
                    with pool.Fori(1, SB) as i:
                        turn(i)

                @block.tensor
                def _(pe):
                    pe.wait_ge(dst_float, 1)
                    for q in range(S):
                        if q >= 2:
                            pe.wait_ge(dst_taken, q - 1)
                        turn_indices(pe, q, q, index_tiles(dst_rows), dst_put)
                    pe.wait_ge(first_float, 1)
                    for c in range(0, G, 512):
                        n = min(512, G - c)
                        last = nc.tensor.matmul(PS[:, 4 + c // 512, 0:n], ones_row[:, :],
                                                base_f[0:1, c:c + n], start=True, stop=True)
                    last.then_inc(base_put, 1)
                    pe.wait_ge(s_w, 16 * WEIGHTS)
                    nc.tensor.transpose(PS[:, 6, 0:D], W3_sb[:, :, :].rearrange("o a i -> o (a i)"),
                                        ident[0:D, 0:D]).then_inc(w3_put, 1)
                    pe.wait_ge(bad_ready, 1)
                    nc.tensor.matmul(PS[0:1, 7, 0:1], bad[:, :], ones_col[:, :], start=True,
                                     stop=True).then_inc(bad_sum, 1)
                    pe.wait_ge(windows_ready, 1)

                    def turn(i):
                        for s in range(S):
                            g = i * S + s
                            rows_at = 2 * (s % 2)
                            reuse(pe, zt_taken, i * S if s < 2 else g - 1)
                            pe.wait_ge(e_loaded[s], i * 16 + 16)
                            pe.wait_ge(gathered[s], i * (16 * TG) + 16 * TG)
                            for j in range(TG):
                                last = nc.tensor.transpose(banks(rows_at, 2, P, EG)[:, j * P:(j + 1) * P],
                                                           Z[:, s, j, :], ident[:, :])
                            last.then_inc(rows_done[s], 1)
                            pe.wait_ge(zt_taken, g + 1)
                            reuse(pe, count_added, i * S + max(s - 1, 0))
                            h = PS[:, 4 + s % 2, 0:HC]
                            for half in (0, 1):
                                lo = half * D
                                nc.tensor.matmul(h[lo:lo + D, 0:2 * P], W1_sb[:, :],
                                                 ZT[:, half * 2 * P:(half + 1) * 2 * P], start=True, stop=True)
                                last = nc.tensor.matmul(h[lo:lo + D, 2 * P:HC], W1_sb[:, :],
                                                        ZT[:, 4 * P + lo:4 * P + lo + D], start=True, stop=True)
                            pe.wait_ge(hot_ready[s], i + 1)
                            for j in range(TG):
                                last = nc.tensor.matmul(PS[0:D, 4 + s % 2, HC:HC + WIN], ones_bf[:, :], hot[:, s, j, :],
                                                        start=(j == 0), stop=(j == TG - 1))
                            last.then_inc(ht_put, 1)
                            if s == 0:
                                reuse(pe, h_ready[S - 2], i)
                            elif s == 1:
                                reuse(pe, h_ready[S - 1], i)
                            else:
                                pe.wait_ge(h_ready[s - 2], i + 1)
                            for j in range(TG):
                                for lo in (0, D):
                                    last = nc.tensor.matmul(PS[lo:lo + D, 6 + s % 2, j * D:(j + 1) * D],
                                                            ZT[:, j * P + lo:j * P + lo + D], W1_sb[:, :],
                                                            start=True, stop=True)
                            last.then_inc(h_put, 1)
                    turn(0)
                    with pe.Fori(1, SB) as i:
                        turn(i)
                    pe.wait_ge(count_added, G)
                    pe.wait_ge(mean_in, 1)
                    nc.tensor.matmul(PS[:, 6, 0:1], halves[:, :], moments[:, 0:1], start=True,
                                     stop=True).then_inc(mean_put, 1)
                    pe.wait_ge(var_in, 1)
                    nc.tensor.matmul(PS[:, 7, 0:1], halves[:, :], var[:, :], start=True,
                                     stop=True).then_inc(var_put, 1)
                    pe.wait_ge(spread_ready, 1)
                    nc.tensor.matmul(PS[:, 5, 0:2 * D], ones_f[:, :], spread[:, :, :].rearrange("p a c -> p (a c)"),
                                     start=True, stop=True).then_inc(rows_put, 1)

                @block.scalar
                def _(act):
                    def store(i, s):
                        act.wait_ge(h_ready[s], i + 1)
                        act.dma_start(h_dram[i * S + s], h_ring[:, s, :, :].rearrange("p t c -> p (t c)")
                                      ).then_inc(h_stored[s], 16)

                    def turn(i):
                        for s in range(S):
                            act.wait_ge(rows_done[s], i + 1)
                            reuse(act, h_put, i * S + s)
                            act.activation(ZT[:, :], banks(2 * (s % 2), 2, P, EG), ACT.Copy).then_inc(zt_taken, 1)
                            if s > 0:
                                store(i, s - 1)
                            elif not isinstance(i, int):
                                store(i - 1, S - 1)

                    turn(0)
                    with act.Fori(1, SB) as i:
                        turn(i)
                    store(SB - 1, S - 1)
                    act.wait_ge(var_sb, 1)
                    act.activation(var[:, :], var[:, :], ACT.Sqrt, bias=epsP[:, :]).then_inc(root1, 1)
                    for s in range(S):
                        act.wait_ge(h_stored[s], 16 * SB)

                @block.vector
                def _(dve):
                    chain = Chain(dve, prep_chain)
                    nc.vector.memset(ones_f[:, :], 1.0)
                    nc.vector.memset(ones_bf[:, :], 1.0)
                    dve.wait_ge(s_dst, 16)
                    nc.vector.tensor_copy(dst_rows[:, :].bitcast(fp32), dst_rows[:, :]).then_inc(dst_float, 1)
                    dve.wait_ge(s_first, 16)
                    nc.vector.tensor_copy(base_row[:, :, 0:S], base_in[:, :].rearrange("o (sb q) -> o sb q", q=S))
                    nc.vector.tensor_copy(base_f[:, :], base_in[:, :]).then_inc(first_float, 1)
                    for q in range(S):
                        dve.wait_ge(dst_put, q + 1)
                        take_indices(q, q, rel5[:, :, :].rearrange("p g j -> p (g j)")).then_inc(dst_taken, 1)
                    dve.wait_ge(dst_taken, S)
                    dve.wait_ge(base_put, 1)
                    chain.link(nc.vector.tensor_copy(base_all[:, :], banks(4, 2, P, G)))
                    chain.link(nc.vector.tensor_tensor(
                        rel5[:, :, :], rel5[:, :, :],
                        base_all[:, :].unsqueeze(2).to_broadcast([P, G, TG]), ALU.subtract))
                    rel_flat = rel5[:, :, :].rearrange("p g j -> p (g j)")
                    nc.vector.reduce_max(most[:, :], rel_flat, AX)
                    chain.link(nc.vector.tensor_reduce(least[:, :], rel_flat, AX, ALU.min))
                    chain.link(nc.vector.tensor_scalar(most[:, :], most[:, :], float(WIN - 1), None, ALU.is_gt))
                    chain.link(nc.vector.tensor_scalar(least[:, :], least[:, :], 0.0, None, ALU.is_lt))
                    nc.vector.tensor_tensor(bad[:, :], most[:, :], least[:, :], ALU.add).then_inc(bad_ready, 1)
                    for c in (0, D):
                        last = nc.vector.tensor_tensor(halves[:, c:c + D], ident[:, 0:D], ident[:, D:P], ALU.add)
                    chain.link(last)
                    nc.vector.tensor_scalar(halves[:, :], halves[:, :], 0.5, None, ALU.mult)
                    dve.wait_ge(w3_put, 1)
                    nc.vector.tensor_copy(W3T[:, :], PS[:, 6, 0:D])
                    dve.wait_ge(bad_sum, 1)
                    chain.link(nc.vector.tensor_scalar(flag_f[:, :], PS[0:1, 7, 0:1], 0.0, None, ALU.is_gt))
                    nc.vector.tensor_copy(flag[:, :], flag_f[:, :]).then_inc(windows_ready, 1)
                    dve.wait_ge(s_w, 16 * WEIGHTS)

                    def turn(i):
                        load_windows(dve, i)
                        firsts = windows_of_turn(dve)
                        for s in range(S):
                            g = i * S + s
                            nc.vector.tensor_tensor(
                                hot[:, s, :, :], window[:, :].unsqueeze(1).to_broadcast([P, TG, WIN]),
                                rel5[:, ds(g, 1), :].rearrange("p a t -> p (a t)").unsqueeze(2)
                                .to_broadcast([P, TG, WIN]), ALU.is_equal).then_inc(hot_ready[s], 1)
                            dve.wait_ge(ht_put, g + 1)
                            nc.vector.bn_stats(stats[:, ds(i * (6 * S) + 6 * s, 6)],
                                               PS[:, 4 + s % 2, 0:HC]).then_inc(stats_done, 1)
                            reuse(dve, count_added, g)
                            nc.vector.tensor_tensor(table[0:D, ds(firsts[s], WIN)], table[0:D, ds(firsts[s], WIN)],
                                                    PS[0:D, 4 + s % 2, HC:HC + WIN], ALU.add).then_inc(count_added, 1)
                            dve.wait_ge(h_put, g + 1)
                            reuse(dve, h_stored[s], i * 16)
                            nc.vector.tensor_tensor(
                                h_ring[:, s, :, :], PS[:, 6 + s % 2, 0:HC].rearrange("p (t c) -> p t c", c=D),
                                b1_row[:, :].unsqueeze(1).to_broadcast([P, TG, D]), ALU.add).then_inc(h_ready[s], 1)
                            nc.vector.tensor_copy(idx_ring[:, s, :],
                                                  src_idx[:, ds(i * (S * TG) + (S + s) * TG, TG)]
                                                  ).then_inc(idx_ready[s], 1)

                    turn(0)
                    with dve.Fori(1, SB) as i:
                        turn(i)
                    chain = Chain(dve, a_chain)
                    dve.wait_ge(stats_done, G)
                    nc.vector.bn_aggr(moments[:, :], stats[:, :]).then_inc(mean_in, 1)
                    dve.wait_ge(mean_put, 1)
                    chain.link(nc.vector.tensor_copy(mean[:, :], PS[:, 6, 0:1]))
                    chain.link(nc.vector.tensor_tensor(off[:, :], moments[:, 0:1], mean[:, :], ALU.subtract))
                    chain.link(nc.vector.tensor_tensor(off[:, :], off[:, :], off[:, :], ALU.mult))
                    nc.vector.tensor_tensor(var[:, :], moments[:, 1:2], off[:, :], ALU.add).then_inc(var_in, 1)
                    dve.wait_ge(var_put, 1)
                    nc.vector.tensor_copy(var[:, :], PS[:, 7, 0:1]).then_inc(var_sb, 1)
                    dve.wait_ge(root1, 1)
                    chain.link(nc.vector.reciprocal(scale_col[:, :], var[:, :]))
                    chain.link(nc.vector.tensor_tensor(scale_col[:, :], scale_col[:, :], g1c[:, :], ALU.mult))
                    chain.link(nc.vector.tensor_tensor(mean[:, :], mean[:, :], b1c[:, :], ALU.add))
                    chain.link(nc.vector.tensor_tensor(off[:, :], mean[:, :], scale_col[:, :], ALU.mult))
                    chain.link(nc.vector.tensor_tensor(shift_col[:, :], be1c[:, :], off[:, :], ALU.subtract))
                    for n, one in enumerate((scale_col, shift_col)):
                        last = nc.vector.tensor_scalar(spread[:, n, :], ident[0:D, 0:D], one[0:D, :], None, ALU.mult)
                    last.then_inc(spread_ready, 1)
                    dve.wait_ge(rows_put, 1)
                    nc.vector.tensor_copy(scale1[:, :], PS[:, 5, 0:D])
                    nc.vector.tensor_copy(shift1[:, :], PS[:, 5, D:2 * D])

        clear_semaphores()

        def pass_b(here):
            h_turns = sb(here, "h_turns", [P, 2, S, HC])
            normed = sb(here, "normed", [P, 2, S * TG, D])
            hot = sb(here, "hot", [P, 2, S * TG, WIN])
            msg = sb(here, "msg", [P, S, TG, D])

            h_loaded = [sem("h_loaded0"), sem("h_loaded1")]
            HOT_STEPS = ((0, 2), (2, 5))
            SCALE_STEPS = ((0, 2), (2, 4), (4, 5))
            scaled = sem("scaled")
            hot_ready = sem("hot_ready")
            shifted = sem("shifted")
            msg_ready = sem("msg_ready")
            summed = sem("summed")
            added = sem("added")

            def tiles_of(s):
                return slice(s * TG, (s + 1) * TG)

            def count_of(i, s, steps):
                return i * len(steps) + 1 + [a <= s < b for a, b in steps].index(True)

            with nc.Block() as block:
                @block.sync
                def _(sp):
                    def turn(i, half, n):
                        if not isinstance(i, int) or i >= 2:
                            sp.wait_ge(scaled, (i - 1) * len(SCALE_STEPS))
                        sp.dma_start(h_turns[:, half, :, :], h_dram[ds(i * S, S)].rearrange("g p c -> p g c")
                                     ).then_inc(h_loaded[half], 16)

                    turn(0, 0, 0)
                    turn(1, 1, 0)
                    loop_halves(sp, 2, SB, turn)

                @block.gpsimd
                def _(pool):
                    def turn(i, half, n):
                        for s in range(S):
                            pool.wait_ge(scaled, count_of(i, s, SCALE_STEPS))
                            rows = normed[:, half, tiles_of(s), :]
                            nc.gpsimd.tensor_tensor(rows, rows, shift1[:, :].unsqueeze(1).to_broadcast([P, TG, D]),
                                                    ALU.add).then_inc(shifted, 1)

                    turn(0, 0, 0)
                    loop_halves(pool, 1, SB, turn)

                @block.scalar
                def _(act):
                    def turn(i, half, n):
                        for s in range(S):
                            act.wait_ge(shifted, i * S + s + 1)
                            if not isinstance(i, int) or i >= 1:
                                act.wait_ge(summed, i * S + (s + 1 - S))
                            act.activation(msg[:, s, :, :], normed[:, half, tiles_of(s), :], ACT.Silu
                                           ).then_inc(msg_ready, 1)

                    turn(0, 0, 0)
                    loop_halves(act, 1, SB, turn)

                @block.tensor
                def _(pe):
                    def turn(i, half, n):
                        for s in range(S):
                            pe.wait_ge(hot_ready, count_of(i, s, HOT_STEPS))
                            pe.wait_ge(msg_ready, i * S + s + 1)
                            if not isinstance(i, int) or i >= 1:
                                pe.wait_ge(added, i * S + (s + 2 - S))
                            for j in range(TG):
                                last = nc.tensor.matmul(PS[D:P, s, 0:WIN], msg[:, s, j, :], hot[:, half, s * TG + j, :],
                                                        start=(j == 0), stop=(j == TG - 1))
                            last.then_inc(summed, 1)

                    turn(0, 0, 0)
                    loop_halves(pe, 1, SB, turn)

                @block.vector
                def _(dve):
                    def one_hot(i, half, a, b):
                        nc.vector.tensor_tensor(
                            hot[:, half, a * TG:b * TG, :],
                            window[:, :].unsqueeze(1).to_broadcast([P, (b - a) * TG, WIN]),
                            rel5[:, ds(i * S + a, b - a), :].rearrange("p g t -> p (g t)").unsqueeze(2)
                            .to_broadcast([P, (b - a) * TG, WIN]), ALU.is_equal).then_inc(hot_ready, 1)

                    def scale(half, a, b):
                        nc.vector.tensor_tensor(normed[:, half, a * TG:b * TG, :],
                                                h_turns[:, half, a:b, :].rearrange("p g (t c) -> p (g t) c", c=D),
                                                scale1[:, :].unsqueeze(1).to_broadcast([P, (b - a) * TG, D]),
                                                ALU.mult).then_inc(scaled, 1)

                    def add(i, s, first):
                        dve.wait_ge(summed, i * S + s + 1)
                        dve.wait_ge(added, i * S + s + 1)
                        nc.vector.tensor_tensor(table[D:P, ds(first, WIN)], table[D:P, ds(first, WIN)],
                                                PS[D:P, s, 0:WIN], ALU.add).then_inc(added, 1)

                    def turn(i, half, n):
                        firsts = windows_of_turn(dve)
                        dve.wait_ge(h_loaded[half], n * 16 + 16)
                        for s, (a, b) in enumerate(SCALE_STEPS):
                            add(i - 1, s, firsts[s])
                            scale(half, a, b)
                        for s, (a, b) in enumerate(HOT_STEPS, len(SCALE_STEPS)):
                            if s == S - 1:
                                load_windows(dve, i)
                            add(i - 1, s, firsts[s])
                            one_hot(i, half, a, b)

                    dve.sem_inc(added, 1)
                    load_windows(dve, 0)
                    dve.wait_ge(h_loaded[0], 16)
                    for a, b in SCALE_STEPS:
                        scale(0, a, b)
                    for a, b in HOT_STEPS:
                        one_hot(0, 0, a, b)
                    loop_halves(dve, 1, SB, turn)
                    for s, first in enumerate(windows_of_turn(dve)):
                        add(SB - 1, s, first)

        with ExitStack() as here:
            pass_b(here)

        def outside(dve, chain, cur, rel, base, parts):
            one = cur[:, 1, :]
            chain.link(nc.vector.tensor_scalar(cur[:, 0, :], rel, 0.0, None, ALU.is_lt))
            chain.link(nc.vector.tensor_scalar(one, rel, float(WIN - 1), None, ALU.is_gt))
            chain.link(nc.vector.tensor_tensor(cur[:, 0, :], cur[:, 0, :], one, ALU.add))
            chain.link(nc.vector.tensor_scalar(one, rel, base, 1.0, ALU.add, ALU.add))
            chain.link(nc.vector.tensor_tensor(cur[:, 0, :], cur[:, 0, :], one, ALU.mult))
            chain.link(nc.vector.tensor_scalar(cur[:, 0, :], cur[:, 0, :], -1.0, None, ALU.add))

        with ExitStack() as here:
            h_slot = sb(here, "h_slot", [P, TG, D])
            msg = sb(here, "msg_g", [P, TG, 2 * D])
            hot = sb(here, "hot_g", [P, TG, WIN])
            cur = sb(here, "cur_g", [P, 2, TG])
            h_in = sem("gb_h_in")
            normed = sem("gb_normed")
            msg_ready = sem("gb_msg_ready")
            hot_ready = sem("gb_hot_ready")
            summed = sem("gb_summed")
            added = sem("gb_added")
            moved_on = sem("gb_moved_on")
            ones_set = sem("gb_ones_set")
            gb_chain = sem("gb_chain")
            with nc.Block() as block:
                @block.sync
                def _(sp):
                    with sp.If(sp.value_load(flag[0:1, 0:1], min_val=0, max_val=1) > 0):
                        with sp.Fori(0, G) as g:
                            sp.wait_ge(msg_ready, g + 1)
                            sp.dma_start(h_slot[:, :, :].rearrange("p t c -> p (t c)"), h_dram[g]).then_inc(h_in, 16)

                @block.scalar
                def _(act):
                    with act.If(act.value_load(flag[0:1, 0:1], min_val=0, max_val=1) > 0):
                        act.sem_inc(msg_ready, 1)
                        with act.Fori(0, G) as g:
                            act.wait_ge(normed, g + 1)
                            act.wait_ge(added, g * NW + 1)
                            act.activation(msg[:, :, D:2 * D], h_slot[:, :, :], ACT.Silu).then_inc(msg_ready, 1)

                @block.tensor
                def _(pe):
                    with pe.If(pe.value_load(flag[0:1, 0:1], min_val=0, max_val=1) > 0):
                        pe.wait_ge(ones_set, 1)
                        pe.sem_inc(summed, 1)
                        with pe.Fori(0, G) as g:
                            pe.wait_ge(msg_ready, g + 2)
                            carry_wait(pe)
                            with pe.Fori(0, NW) as w:
                                pe.wait_ge(hot_ready, g * NW + w + 1)
                                pe.wait_ge(added, g * NW + w + 1)
                                for j in range(TG):
                                    last = nc.tensor.matmul(PS[:, 1, 0:WIN], msg[:, j, :], hot[:, j, :],
                                                            start=(j == 0), stop=(j == TG - 1))
                                last.then_inc(summed, 1)

                @block.vector
                def _(dve):
                    with dve.If(dve.value_load(flag[0:1, 0:1], min_val=0, max_val=1) > 0):
                        nc.vector.memset(msg[:, :, 0:D], 1.0).then_inc(ones_set, 1)
                        dve.sem_inc(added, 1)
                        dve.sem_inc(moved_on, 1)
                        with dve.Fori(0, G) as g:
                            chain = Chain(dve, gb_chain, g * 7)
                            dve.wait_ge(h_in, g * 16 + 16)
                            chain.link(nc.vector.tensor_tensor(
                                h_slot[:, :, :], h_slot[:, :, :],
                                scale1[:, :].unsqueeze(1).to_broadcast([P, TG, D]), ALU.mult))
                            nc.vector.tensor_tensor(
                                h_slot[:, :, :], h_slot[:, :, :],
                                shift1[:, :].unsqueeze(1).to_broadcast([P, TG, D]), ALU.add).then_inc(normed, 1)
                            dve.wait_ge(moved_on, g * NW + 1)
                            outside(dve, chain, cur, rel5[:, ds(g, 1), :].rearrange("p a t -> p (a t)"),
                                    base_all[:, ds(g, 1)], P)
                            carry_wait(dve)
                            with dve.Fori(0, NW) as w:
                                dve.wait_ge(summed, g * NW + w + 1)
                                dve.wait_ge(moved_on, g * NW + w + 1)
                                nc.vector.tensor_tensor(
                                    hot[:, :, :], window[:, :].unsqueeze(1).to_broadcast([P, TG, WIN]),
                                    cur[:, 0, :].unsqueeze(2).to_broadcast([P, TG, WIN]),
                                    ALU.is_equal).then_inc(hot_ready, 1)
                                dve.wait_ge(hot_ready, g * NW + w + 1)
                                nc.vector.tensor_scalar(cur[:, 0, :], cur[:, 0, :], -float(WIN), None,
                                                        ALU.add).then_inc(moved_on, 1)
                                dve.wait_ge(summed, g * NW + w + 2)
                                dve.wait_ge(added, g * NW + w + 1)
                                nc.vector.tensor_tensor(table[:, ds(w * WIN, WIN)], table[:, ds(w * WIN, WIN)],
                                                        PS[:, 1, 0:WIN], ALU.add).then_inc(added, 1)

        wide_z = [NP, PT, D]

        def norm_sems(name):
            return {n: sem(f"{name}_{n}") for n in ("z_ready", "chain", "centered", "squared", "var_ready",
                                                    "root_done")}

        def norm_vector(dve, turned, sm, square, mean, var):
            def moment(i):
                dve.wait_ge(sm["squared"], i + 1)
                carry_wait(dve)
                nc.vector.reduce_sum(var[:, ds(i * PT, PT)], square[:, :, :], AX).then_inc(sm["var_ready"], 1)

            def turn(i):
                z = x3[:, ds(i * PT, PT), :]
                chain = Chain(dve, sm["chain"], i * 2)
                dve.wait_ge(turned[S - 1], i + 1)
                nc.vector.tensor_tensor(z, z, banks(0, 3, NP, PT * D).rearrange("p (t c) -> p t c", c=D),
                                        ALU.add).then_inc(sm["z_ready"], 1)
                dve.wait_ge(sm["z_ready"], i + 1)
                carry_wait(dve)
                chain.link(nc.vector.reduce_sum(mean[:, :], z, AX))
                chain.link(nc.vector.tensor_scalar(mean[:, :], mean[:, :], 1.0 / D, None, ALU.mult))
                nc.vector.tensor_tensor(z, z, mean[:, :].unsqueeze(2).to_broadcast(wide_z),
                                        ALU.subtract).then_inc(sm["centered"], 1)
                if not isinstance(i, int):
                    moment(i - 1)
                dve.wait_ge(sm["centered"], i + 1)

            turn(0)
            with dve.Fori(1, PIECES) as i:
                turn(i)
            moment(PIECES - 1)
            dve.wait_ge(sm["root_done"], 1)
            Chain(dve, sm["chain"], 2 * PIECES).link(nc.vector.reciprocal(var[:, :], var[:, :]))

        def norm_act(act, sm, square, var, activations):
            def squares(i):
                act.wait_ge(sm["centered"], i + 1)
                reuse(act, sm["var_ready"], i)
                carry_wait(act)
                act.activation(square[:, :, :], x3[:, ds(i * PT, PT), :], ACT.Square).then_inc(sm["squared"], 1)

            activations(0)
            activations(1)
            squares(0)
            with act.Fori(2, PIECES) as i:
                activations(i)
                squares(i - 1)
            squares(PIECES - 1)
            act.wait_ge(sm["var_ready"], PIECES)
            act.activation(var[:, :], var[:, :], ACT.Sqrt, bias=epsP[0:NP, :], scale=1.0 / D
                           ).then_inc(sm["root_done"], 1)

        def norm_turn_back(pe, i, s, sm, act_ring, act_ready, act_turned):
            if s == 0:
                reuse(pe, sm["z_ready"], i)
            pe.wait_ge(act_ready[s], i + 1)
            carry_wait(pe)
            for t in range(CT):
                n = s * CT + t
                last = nc.tensor.transpose(banks(0, 3, NP, PT * D)[:, n * D:(n + 1) * D],
                                           act_ring[:, s, t * NP:(t + 1) * NP], ident[0:D, 0:D])
            last.then_inc(act_turned[s], 1)

        clear_semaphores()

        with ExitStack() as here:
            QUARTER = NODES // 4
            x_ring = sb(here, "x_ring", [NP, S, CT, D])
            counts = sb(here, "counts", [NP, NT])
            shares = sb(here, "shares", [P, 4, QUARTER])
            stats = sb(here, "stats_n", [D, CHUNKS * 6])
            moments = sb(here, "moments_n", [D, 2])
            root = sb(here, "root_n", [D, 1])
            act_ring = sb(here, "act_ring", [D, S, CN])
            square = sb(here, "square_n", [NP, PT, D])
            mean_z = sb(here, "mean_z_n", [NP, PT])
            var_z = sb(here, "var_z_n", [NP, NT])
            x1_halves = [sb(here, "x1_n", [NP, PT, D]), square]
            eps1c = sb(here, "eps1c", [P, 1])

            x_loaded = sems("x_loaded")
            x_turned = sems("x_turned")
            counts_out = sem("counts_out")
            counts_in = sem("counts_in")
            shares_made = sem("shares_made")
            shares_out = sem("shares_out")
            shares_in = [sem(f"shares_in{n}") for n in range(4)]
            means_done = sem("means_done")
            last_mean_done = sem("last_mean_done")
            count_chain = sem("count_chain")
            xT_ready = sems("xT_ready")
            h2_put = sem("h2_put")
            h2_ready = sem("h2_ready")
            h2_stats = sem("h2_stats")
            n_chain = sem("n_chain")
            var2_in = sem("var2_in")
            root2 = sem("root2")
            bn2_ready = sem("bn2_ready")
            act_ready = sems("act_ready")
            act_turned = sems("act_turned")
            norm_n = norm_sems("norm_n")
            x1_ready = sems("x1_ready")
            x1_stored = [sems("x1_stored_a"), sems("x1_stored_b")]
            x1_turned = sems("x1_turned")
            x1T_ready = sems("x1T_ready")

            ODD_BY_DVE = (0, 1, 2)

            def x1_tiles(half, s, a, b):
                return x1_halves[half][:, s * CT + a:s * CT + b, :]

            def x_rows(i, s, odd):
                return table_t[0:D, ds((i * S + s) * CT, CT), :].rearrange("f (u a) p -> f u a p", a=2)[:, :, odd, :]

            def x_put(s, odd):
                return PS[odd * D:(odd + 1) * D, s, 0:2 * NP].rearrange("f (u p) -> f u p", p=NP)

            with nc.Block() as block:
                @block.sync
                def _(sp):
                    def turn(i):
                        for s in range(S):
                            reuse(sp, x_turned[s], i)
                            sp.dma_start(x_ring[:, s, :, :], x_v[:, ds((i * S + s) * CT, CT), :]
                                         ).then_inc(x_loaded[s], 16)

                    turn(0)
                    with sp.Fori(1, PIECES) as i:
                        turn(i)
                    def turn(i, half, n):
                        for s in range(S):
                            sp.wait_ge(x1_ready[s], i + 1)
                            sp.dma_start(x1_v[:, ds((i * S + s) * (CT * D), CT * D)],
                                         x1_tiles(half, s, 0, CT).rearrange("p t c -> p (t c)")
                                         ).then_inc(x1_stored[half][s], 16)

                    turn(0, 0, 0)
                    loop_halves(sp, 1, PIECES, turn)
                    for s in range(S):
                        sp.wait_ge(x1_stored[0][s], 16 * ((PIECES + 1) // 2))
                        sp.wait_ge(x1_stored[1][s], 16 * (PIECES // 2))

                @block.gpsimd
                def _(pool):
                    pool.dma_start(counts_dram.rearrange("(o n) -> o n", o=1), table[0:1, 0:NODES]).then_inc(counts_out, 16)
                    pool.wait_ge(counts_out, 16)
                    pool.dma_start(counts[:, :], counts_dram.rearrange("(p t) -> p t", p=NP)).then_inc(counts_in, 16)
                    pool.wait_ge(shares_made, 1)
                    pool.dma_start(shares_dram.rearrange("(p t) -> p t", p=NP), counts[:, :]).then_inc(shares_out, 16)
                    pool.wait_ge(shares_out, 16)
                    for n in (3, 0, 1, 2):
                        pool.dma_start(shares[D:P, n, :],
                                       shares_dram[n * QUARTER:(n + 1) * QUARTER].partition_broadcast(D)
                                       ).then_inc(shares_in[n], 16)
                    sums = table[D:P, 3 * QUARTER:NODES]
                    pool.wait_ge(shares_in[3], 16)
                    nc.gpsimd.tensor_tensor(sums, sums, shares[D:P, 3, :], ALU.mult).then_inc(last_mean_done, 1)
                    pool.wait_ge(h2_put, CHUNKS)
                    nc.gpsimd.memset(table[D:P, :], 0.0)

                @block.tensor
                def _(pe):
                    def turn(i):
                        for s in range(S):
                            pe.wait_ge(x_loaded[s], i * 16 + 16)
                            reuse(pe, xT_ready[s], i * 2)
                            carry_wait(pe)
                            for u in range(2):
                                last = nc.tensor.transpose(PS[:, s, u * NP:(u + 1) * NP],
                                                           x_ring[:, s, 2 * u:2 * u + 2, :].rearrange("p t c -> p (t c)"),
                                                           ident[0:NP, 0:NP])
                            last.then_inc(x_turned[s], 1)

                    turn(0)
                    with pe.Fori(1, PIECES) as i:
                        turn(i)
                    pe.wait_ge(means_done, 3)
                    pe.wait_ge(last_mean_done, 1)
                    for s in range(S):
                        pe.wait_ge(xT_ready[s], 2 * PIECES)
                    def turn(i):
                        for s in range(S):
                            if not isinstance(i, int):
                                pe.wait_ge(h2_ready, (i - 1) * S + s + 1)
                            nc.tensor.matmul(PS[0:D, s, 0:CN].rearrange("f (t p) -> f t p", t=CT),
                                             W2_sb[:, :], table_t[:, ds((i * S + s) * CT, CT), :],
                                             start=True, stop=True).then_inc(h2_put, 1)

                    turn(0)
                    with pe.Fori(1, PIECES) as i:
                        turn(i)
                    pe.wait_ge(h2_ready, CHUNKS)
                    def turn(i):
                        for s in range(S):
                            norm_turn_back(pe, i, s, norm_n, act_ring, act_ready, act_turned)

                    turn(0)
                    with pe.Fori(1, PIECES) as i:
                        turn(i)
                    pe.wait_ge(norm_n["z_ready"], PIECES)
                    def turn(i, half, n):
                        for s in range(S):
                            pe.wait_ge(x1_ready[s], i + 1)
                            reuse(pe, x1T_ready[s], i * 2)
                            carry_wait(pe)
                            for u in range(2):
                                last = nc.tensor.transpose(PS[:, s, u * NP:(u + 1) * NP],
                                                           x1_tiles(half, s, 2 * u, 2 * u + 2)
                                                           .rearrange("p t c -> p (t c)"), ident[0:NP, 0:NP])
                            last.then_inc(x1_turned[s], 1)

                    turn(0, 0, 0)
                    loop_halves(pe, 1, PIECES, turn)

                @block.scalar
                def _(act):
                    act.wait_ge(counts_out, 16)
                    def turn(i):
                        for s in range(S):
                            act.wait_ge(x_turned[s], i + 1)
                            carry_wait(act)
                            for odd in range(2):
                                act.activation(x_rows(i, s, odd), x_put(s, odd), ACT.Copy).then_inc(xT_ready[s], 1)

                    turn(0)
                    with act.Fori(1, PIECES) as i:
                        turn(i)
                    def turn(i):
                        for s in range(S):
                            act.wait_ge(h2_put, i * S + s + 1)
                            carry_wait(act)
                            act.activation(table_t[0:D, ds((i * S + s) * CT, CT), :],
                                           PS[0:D, s, 0:CN].rearrange("f (t p) -> f t p", t=CT),
                                           ACT.Identity, bias=b2c[:, :]).then_inc(h2_ready, 1)

                    turn(0)
                    with act.Fori(1, PIECES) as i:
                        turn(i)
                    act.wait_ge(var2_in, 1)
                    act.activation(root[:, :], moments[:, 1:2], ACT.Sqrt, bias=epsP[0:D, :]).then_inc(root2, 1)
                    act.wait_ge(bn2_ready, 1)
                    def silu(i):
                        for s in range(S):
                            reuse(act, act_turned[s], i)
                            carry_wait(act)
                            act.activation(act_ring[:, s, :].rearrange("f (t p) -> f t p", t=CT),
                                           table_t[0:D, ds((i * S + s) * CT, CT), :], ACT.Silu,
                                           bias=shift2[:, :], scale=scale2[:, :]).then_inc(act_ready[s], 1)

                    norm_act(act, norm_n, square, var_z, silu)
                    def turn(i):
                        for s in range(S):
                            act.wait_ge(x1_turned[s], i + 1)
                            carry_wait(act)
                            for odd in range(1 if s in ODD_BY_DVE else 2):
                                act.activation(x_rows(i, s, odd), x_put(s, odd), ACT.Identity,
                                               scale=eps1c[odd * D:(odd + 1) * D, :]).then_inc(x1T_ready[s], 1)

                    turn(0)
                    with act.Fori(1, PIECES) as i:
                        turn(i)

                @block.vector
                def _(dve):
                    chain = Chain(dve, count_chain)
                    nc.vector.tensor_scalar(eps1c[:, :], eps_c[:, :], 1.0, None, ALU.add)
                    dve.wait_ge(counts_in, 16)
                    chain.link(nc.vector.tensor_scalar(counts[:, :], counts[:, :], 1.0, None, ALU.max))
                    nc.vector.reciprocal(counts[:, :], counts[:, :]).then_inc(shares_made, 1)
                    for n in range(3):
                        sums = table[D:P, n * QUARTER:(n + 1) * QUARTER]
                        dve.wait_ge(shares_in[n], 16)
                        nc.vector.tensor_tensor(sums, sums, shares[D:P, n, :], ALU.mult).then_inc(means_done, 1)
                    def turn(i):
                        for s in range(S):
                            k = i * S + s
                            dve.wait_ge(h2_ready, k + 1)
                            nc.vector.bn_stats(stats[:, ds(k * 6, 6)], table_t[0:D, ds(k * CT, CT), :]
                                               ).then_inc(h2_stats, 1)

                    turn(0)
                    with dve.Fori(1, PIECES) as i:
                        turn(i)
                    dve.wait_ge(h2_stats, CHUNKS)
                    nc.vector.bn_aggr(moments[:, :], stats[:, :]).then_inc(var2_in, 1)
                    dve.wait_ge(root2, 1)
                    chain = Chain(dve, n_chain)
                    chain.link(nc.vector.reciprocal(root[:, :], root[:, :]))
                    chain.link(nc.vector.tensor_tensor(scale2[:, :], root[:, :], g2c[:, :], ALU.mult))
                    chain.link(nc.vector.tensor_tensor(root[:, :], moments[:, 0:1], scale2[:, :], ALU.mult))
                    nc.vector.tensor_tensor(shift2[:, :], be2c[:, :], root[:, :], ALU.subtract).then_inc(bn2_ready, 1)

                    norm_vector(dve, act_turned, norm_n, square, mean_z, var_z)
                    def turn(i, half, n):
                        for s in range(S):
                            tiles = ds((i * S + s) * CT, CT)
                            if not isinstance(i, int) or i >= 2:
                                dve.wait_ge(x1_turned[s], i - 1)
                                dve.wait_ge(x1_stored[half][s], n * 16)
                            nc.vector.tensor_tensor(x1_tiles(half, s, 0, CT), x3[:, tiles, :],
                                                    var_z[:, tiles].unsqueeze(2).to_broadcast([NP, CT, D]),
                                                    ALU.mult).then_inc(x1_ready[s], 1)
                            if s - 2 in ODD_BY_DVE:
                                dve.wait_ge(x1_turned[s - 2], i + 1)
                                nc.vector.tensor_scalar(x_rows(i, s - 2, 1), x_put(s - 2, 1), eps1c[D:P, :], None,
                                                        ALU.mult).then_inc(x1T_ready[s - 2], 1)

                    turn(0, 0, 0)
                    turn(1, 1, 0)
                    loop_halves(dve, 2, PIECES, turn)

        clear_semaphores()

        with ExitStack() as here:
            E = sb(here, "E", [P, S, TG, D])
            X = sb(here, "X", [P, S, TG, D])
            msg = sb(here, "msg_c", [P, S, TG, D])
            hot = sb(here, "hot_c", [P, S, TG, WIN])
            e_loaded = sems("c_e_loaded")
            gathered = gathered_x1
            sum_ready = sems("sum_ready")
            idx_ready = sems("c_idx_ready")
            hot_ready = sems("c_hot_ready")
            msg_ready = sems("c_msg_ready")
            summed = sems("c_summed")
            added = sem("c_added")
            idx_first = sem("idx_first")
            x1_kept = sem("x1_kept")

            with nc.Block() as block:
                @block.sync
                def _(sp):
                    def turn(i):
                        for s in range(S):
                            reuse(sp, msg_ready[s], i)
                            sp.dma_start(E[:, s, :, :], edge_v[i * S + s]).then_inc(e_loaded[s], 16)

                    turn(0)
                    sp.dma_start(x_nodes[:, :], x1_v).then_inc(x1_kept, 16)
                    with sp.Fori(1, SB) as i:
                        turn(i)
                    sp.wait_ge(x1_kept, 16)

                @block.gpsimd
                def _(pool):
                    pool.wait_ge(idx_first, 1)
                    def turn(i):
                        for s in range(S):
                            reuse(pool, idx_ready[s], i)
                            reuse(pool, sum_ready[s], i)
                            carry_wait(pool)
                            for j in range(TG):
                                nc.gpsimd.indirect_dma_start(
                                    out=X[:, s, j, :], out_offset=None, in_=x1_dram,
                                    in_offset=bass.IndirectOffsetOnAxis(ap=idx_ring[:, s, j:j + 1], axis=0)
                                ).then_inc(gathered[s], 16)

                    turn(0)
                    with pool.Fori(1, SB) as i:
                        turn(i)

                @block.scalar
                def _(act):
                    def turn(i):
                        for s in range(S):
                            act.wait_ge(sum_ready[s], i + 1)
                            reuse(act, summed[s], i)
                            act.activation(msg[:, s, :, :], E[:, s, :, :], ACT.Relu).then_inc(msg_ready[s], 1)

                    turn(0)
                    with act.Fori(1, SB) as i:
                        turn(i)

                @block.tensor
                def _(pe):
                    def turn(i):
                        for s in range(S):
                            pe.wait_ge(msg_ready[s], i + 1)
                            pe.wait_ge(hot_ready[s], i + 1)
                            reuse(pe, added, i * S + max(s - 1, 0))
                            for j in range(TG):
                                last = nc.tensor.matmul(PS[D:P, s % 2, 0:WIN], msg[:, s, j, :], hot[:, s, j, :],
                                                        start=(j == 0), stop=(j == TG - 1))
                            last.then_inc(summed[s], 1)

                    turn(0)
                    with pe.Fori(1, SB) as i:
                        turn(i)

                @block.vector
                def _(dve):
                    nc.vector.tensor_copy(idx_flat, src_idx[:, 0:S * TG]).then_inc(idx_first, 1)
                    def turn(i):
                        load_windows(dve, i)
                        firsts = windows_of_turn(dve)
                        for s in range(S):
                            g = i * S + s
                            reuse(dve, summed[s], i)
                            nc.vector.tensor_tensor(
                                hot[:, s, :, :], window[:, :].unsqueeze(1).to_broadcast([P, TG, WIN]),
                                rel5[:, ds(g, 1), :].rearrange("p a t -> p (a t)").unsqueeze(2)
                                .to_broadcast([P, TG, WIN]), ALU.is_equal).then_inc(hot_ready[s], 1)
                            dve.wait_ge(e_loaded[s], i * 16 + 16)
                            dve.wait_ge(gathered[s], i * (16 * TG) + 16 * TG)
                            nc.vector.tensor_tensor(E[:, s, :, :], X[:, s, :, :], E[:, s, :, :],
                                                    ALU.add).then_inc(sum_ready[s], 1)
                            nc.vector.tensor_copy(idx_ring[:, s, :],
                                                  src_idx[:, ds(i * (S * TG) + (S + s) * TG, TG)]
                                                  ).then_inc(idx_ready[s], 1)
                            dve.wait_ge(summed[s], i + 1)
                            reuse(dve, added, g)
                            nc.vector.tensor_tensor(table[D:P, ds(firsts[s], WIN)], table[D:P, ds(firsts[s], WIN)],
                                                    PS[D:P, s % 2, 0:WIN], ALU.add).then_inc(added, 1)

                    turn(0)
                    with dve.Fori(1, SB) as i:
                        turn(i)

        with ExitStack() as here:
            E = sb(here, "E_g", [P, TG, D])
            X = sb(here, "X_g", [P, TG, D])
            msg = sb(here, "msg_h", [P, TG, D])
            hot = sb(here, "hot_h", [P, TG, WIN])
            cur = sb(here, "cur_h", [P, 2, TG])
            e_in = sem("gc_e_in")
            idx_in = sem("gc_idx_in")
            rows_in = gathered_general
            sum_in = sem("gc_sum_in")
            msg_ready = sem("gc_msg_ready")
            hot_ready = sem("gc_hot_ready")
            summed = sem("gc_summed")
            added = sem("gc_added")
            moved_on = sem("gc_moved_on")
            gc_chain = sem("gc_chain")
            with nc.Block() as block:
                @block.sync
                def _(sp):
                    with sp.If(sp.value_load(flag[0:1, 0:1], min_val=0, max_val=1) > 0):
                        with sp.Fori(0, G) as g:
                            sp.wait_ge(msg_ready, g + 1)
                            sp.dma_start(E[:, :, :], edge_v[g]).then_inc(e_in, 16)

                @block.gpsimd
                def _(pool):
                    with pool.If(pool.value_load(flag[0:1, 0:1], min_val=0, max_val=1) > 0):
                        with pool.Fori(0, G) as g:
                            pool.wait_ge(idx_in, g + 1)
                            carry_wait(pool)
                            for j in range(TG):
                                nc.gpsimd.indirect_dma_start(
                                    out=X[:, j, :], out_offset=None, in_=x1_dram,
                                    in_offset=bass.IndirectOffsetOnAxis(ap=idx_ring[:, 0, j:j + 1], axis=0)
                                ).then_inc(rows_in, 16)

                @block.scalar
                def _(act):
                    with act.If(act.value_load(flag[0:1, 0:1], min_val=0, max_val=1) > 0):
                        act.sem_inc(msg_ready, 1)
                        with act.Fori(0, G) as g:
                            act.wait_ge(sum_in, g + 1)
                            act.wait_ge(added, g * NW + 1)
                            act.activation(msg[:, :, :], E[:, :, :], ACT.Relu).then_inc(msg_ready, 1)

                @block.tensor
                def _(pe):
                    with pe.If(pe.value_load(flag[0:1, 0:1], min_val=0, max_val=1) > 0):
                        pe.sem_inc(summed, 1)
                        with pe.Fori(0, G) as g:
                            pe.wait_ge(msg_ready, g + 2)
                            carry_wait(pe)
                            with pe.Fori(0, NW) as w:
                                pe.wait_ge(hot_ready, g * NW + w + 1)
                                pe.wait_ge(added, g * NW + w + 1)
                                for j in range(TG):
                                    last = nc.tensor.matmul(PS[D:P, 1, 0:WIN], msg[:, j, :], hot[:, j, :],
                                                            start=(j == 0), stop=(j == TG - 1))
                                last.then_inc(summed, 1)

                @block.vector
                def _(dve):
                    with dve.If(dve.value_load(flag[0:1, 0:1], min_val=0, max_val=1) > 0):
                        dve.sem_inc(added, 1)
                        dve.sem_inc(moved_on, 1)
                        with dve.Fori(0, G) as g:
                            nc.vector.tensor_copy(idx_ring[:, 0, :], src_idx[:, ds(g * TG, TG)]).then_inc(idx_in, 1)
                            dve.wait_ge(e_in, g * 16 + 16)
                            dve.wait_ge(rows_in, g * (16 * TG) + 16 * TG)
                            nc.vector.tensor_tensor(E[:, :, :], X[:, :, :], E[:, :, :], ALU.add).then_inc(sum_in, 1)
                            chain = Chain(dve, gc_chain, g * 6)
                            dve.wait_ge(moved_on, g * NW + 1)
                            outside(dve, chain, cur, rel5[:, ds(g, 1), :].rearrange("p a t -> p (a t)"),
                                    base_all[:, ds(g, 1)], P)
                            carry_wait(dve)
                            with dve.Fori(0, NW) as w:
                                dve.wait_ge(summed, g * NW + w + 1)
                                dve.wait_ge(moved_on, g * NW + w + 1)
                                nc.vector.tensor_tensor(
                                    hot[:, :, :], window[:, :].unsqueeze(1).to_broadcast([P, TG, WIN]),
                                    cur[:, 0, :].unsqueeze(2).to_broadcast([P, TG, WIN]),
                                    ALU.is_equal).then_inc(hot_ready, 1)
                                dve.wait_ge(hot_ready, g * NW + w + 1)
                                nc.vector.tensor_scalar(cur[:, 0, :], cur[:, 0, :], -float(WIN), None,
                                                        ALU.add).then_inc(moved_on, 1)
                                dve.wait_ge(summed, g * NW + w + 2)
                                dve.wait_ge(added, g * NW + w + 1)
                                nc.vector.tensor_tensor(table[D:P, ds(w * WIN, WIN)], table[D:P, ds(w * WIN, WIN)],
                                                        PS[D:P, 1, 0:WIN], ALU.add).then_inc(added, 1)

        clear_semaphores()

        with ExitStack() as here:
            act_ring = sb(here, "act_ring_o", [D, S, CN])
            square = sb(here, "square_o", [NP, PT, D])
            mean_z = sb(here, "mean_z_o", [NP, PT])
            var_z = sb(here, "var_z_o", [NP, NT])
            lin_put = sems("lin_put")
            act_ready = sems("o_act_ready")
            act_turned = sems("o_act_turned")
            norm_o = norm_sems("norm_o")
            y_ready = sem("y_ready")
            y_stored = sem("y_stored")
            with nc.Block() as block:
                @block.sync
                def _(sp):
                    def turn(i):
                        sp.wait_ge(y_ready, i + 1)
                        sp.dma_start(out_v[:, ds(i * (PT * D), PT * D)],
                                     x_nodes[:, ds(i * (PT * D), PT * D)]).then_inc(y_stored, 16)

                    turn(0)
                    with sp.Fori(1, PIECES) as i:
                        turn(i)
                    sp.wait_ge(y_stored, 16 * PIECES)

                @block.tensor
                def _(pe):
                    def linear(i, s):
                        reuse(pe, act_ready[s], i)
                        nc.tensor.matmul(PS[0:D, 3 + s, 0:CN].rearrange("f (t p) -> f t p", t=CT), W3T[:, :],
                                         table_t[:, ds((i * S + s) * CT, CT), :],
                                         start=True, stop=True).then_inc(lin_put[s], 1)

                    def back(i, s):
                        norm_turn_back(pe, i, s, norm_o, act_ring, act_ready, act_turned)

                    for s in range(S):
                        linear(0, s)
                    for s in range(S):
                        linear(1, s)
                        back(0, s)
                    with pe.Fori(2, PIECES) as i:
                        for s in range(S):
                            linear(i, s)
                            back(i - 1, s)
                    for s in range(S):
                        back(PIECES - 1, s)

                @block.scalar
                def _(act):
                    def relu(i):
                        for s in range(S):
                            act.wait_ge(lin_put[s], i + 1)
                            reuse(act, act_turned[s], i)
                            act.activation(act_ring[:, s, :], PS[0:D, 3 + s, 0:CN], ACT.Relu,
                                           bias=b3c[:, :]).then_inc(act_ready[s], 1)

                    norm_act(act, norm_o, square, var_z, relu)

                @block.vector
                def _(dve):
                    norm_vector(dve, act_turned, norm_o, square, mean_z, var_z)
                    def turn(i):
                        y = x3[:, ds(i * PT, PT), :]
                        nc.vector.tensor_tensor(y, y, var_z[:, ds(i * PT, PT)].unsqueeze(2).to_broadcast(wide_z),
                                                ALU.mult).then_inc(y_ready, 1)

                    turn(0)
                    with dve.Fori(1, PIECES) as i:
                        turn(i)


_INS = ['x', 'src', 'dst', 'edge_attr_64', 'L0_gnn_W1', 'L0_gnn_b1', 'L0_gnn_g1', 'L0_gnn_be1',
        'L0_gnn_W2', 'L0_gnn_b2', 'L0_gnn_g2', 'L0_gnn_be2', 'L1_gnn_W', 'L1_gnn_b', 'L1_gnn_eps']


def kernel(**inputs):
    import numpy as _np
    import concourse.bacc as _bacc
    from concourse import mybir as _mybir
    from concourse.bass_utils import run_bass_kernel_spmd as _run

    nc = _bacc.Bacc("TRN2", target_bir_lowering=False, num_devices=1)
    arrays, args = {}, []
    for name in _INS:
        a = _np.ascontiguousarray(inputs[name])
        if a.ndim == 0:
            a = a.reshape(1)
        arrays[f"in_{name}_dram"] = a
        args.append(nc.dram_tensor(f"in_{name}_dram", a.shape, _mybir.dt.from_np(a.dtype), kind="ExternalInput").ap())
    args.append(nc.dram_tensor("out_dram", inputs["x"].shape, _mybir.dt.float32, kind="ExternalOutput").ap())
    gnn_kernel(nc, *args)
    r = _run(nc, [arrays], core_ids=[0])
    return r.results[0]["out_dram"]
```
